# Optimizing a Trainium2 kernel written in Bass

```python
import numpy as np
import jax
import jax.numpy as jnp

def _softmax(x, axis=-1):
    return jax.nn.softmax(x, axis=axis)

def _gelu(x):
    return jax.nn.gelu(x, approximate=True)

def _silu(x):
    return jax.nn.silu(x)

def _sigmoid(x):
    return jax.nn.sigmoid(x)

def _layernorm(x, axis=-1, eps=1e-05):
    m = jnp.mean(x, axis=axis, keepdims=True)
    v = jnp.var(x, axis=axis, keepdims=True)
    return (x - m) / jnp.sqrt(v + eps)

def _scatter_add(tgt, idx, src, axis=0):
    return tgt.at[idx].add(src)

def _segment_sum(src, seg, n):
    return jax.ops.segment_sum(src, seg, n)
kernel_name = 'mk_gnn_preln_d1_gnn_r8_10062d'

def setup_inputs(seed: int=0):
    np.random.seed(seed)
    _w = jnp.asarray

    def _rec_inputs():
        import jax
        import jax.numpy as jnp
        _gk = jax.random.key(seed)
        x = -0.0003713 + 1 * jax.random.normal(jax.random.fold_in(_gk, 1), (6250, 256), jnp.float32)
        _s = jax.random.randint(jax.random.fold_in(_gk, 2), (50000,), 0, 6250, jnp.int32)
        _d = jax.random.randint(jax.random.fold_in(_gk, 3), (50000,), 0, 6250, jnp.int32)
        _loop = jnp.arange(6250, dtype=jnp.int32)
        src = jnp.concatenate([_s, _d, _loop])
        dst = jnp.concatenate([_d, _s, _loop])
        _o = jnp.argsort(dst, stable=True)
        src = src[_o]
        dst = dst[_o]
        edge_attr_96 = -4.21973e-05 + 0.999841 * jax.random.normal(jax.random.fold_in(_gk, 12), (106250, 96), jnp.float32)
        return (x, src, dst, edge_attr_96)
    x, src, dst, edge_attr_96 = _rec_inputs()

    def _L0_gnn_setup():
        import jax, jax.numpy as jnp
        import numpy as np
        N_NODES = 6250
        N_EDGES = 100000
        EDGE_F = 96
        NODE_F = 256
        GLOB_F = 64
        HIDDEN = 1024
        N_GRAPHS = 8
        MLP_IN = NODE_F + 3 * EDGE_F + GLOB_F
        key = jax.random.key(seed)
        ks = jax.random.split(key, 9)
        x = jax.random.normal(ks[0], (N_NODES, NODE_F), dtype=jnp.float32)
        edge_attr = jax.random.normal(ks[1], (N_EDGES, EDGE_F), dtype=jnp.float32)
        u = jax.random.normal(ks[2], (N_GRAPHS, GLOB_F), dtype=jnp.float32)
        W1 = jax.random.normal(ks[3], (MLP_IN, HIDDEN), dtype=jnp.float32) * (1.0 / np.sqrt(MLP_IN))
        b1 = jax.random.normal(ks[4], (HIDDEN,), dtype=jnp.float32) * 0.01
        W2 = jax.random.normal(ks[5], (HIDDEN, NODE_F), dtype=jnp.float32) * (1.0 / np.sqrt(HIDDEN))
        b2 = jax.random.normal(ks[6], (NODE_F,), dtype=jnp.float32) * 0.01
        edge_index = jax.random.randint(ks[7], (2, N_EDGES), 0, N_NODES, dtype=jnp.int64 if jax.config.jax_enable_x64 else jnp.int32)
        batch = jnp.sort(jax.random.randint(ks[8], (N_NODES,), 0, N_GRAPHS, dtype=jnp.int32))
        return {'x': x, 'edge_attr': edge_attr, 'u': u, 'W1': W1, 'b1': b1, 'W2': W2, 'b2': b2, 'edge_index': edge_index, 'batch': batch}
    _L0_gnn_all = _L0_gnn_setup()
    _L0_gnn_in = {k: v for k, v in _L0_gnn_all.items() if k in ('u', 'W1', 'b1', 'W2', 'b2')}
    del _L0_gnn_all
    return {'x': x, 'src': src, 'dst': dst, 'edge_attr_96': edge_attr_96, 'L0_gnn_u': _L0_gnn_in['u'], 'L0_gnn_W1': _L0_gnn_in['W1'], 'L0_gnn_b1': _L0_gnn_in['b1'], 'L0_gnn_W2': _L0_gnn_in['W2'], 'L0_gnn_b2': _L0_gnn_in['b2']}

def reference(x, src, dst, edge_attr_96, L0_gnn_u, L0_gnn_W1, L0_gnn_b1, L0_gnn_W2, L0_gnn_b2):
    import jax
    import jax.numpy as jnp

    def _L0_gnn_ref(x, edge_attr, u, W1, b1, W2, b2, edge_index, batch):
        import jax, jax.numpy as jnp
        import numpy as np
        N_NODES = 6250
        N_EDGES = 100000
        EDGE_F = 96
        NODE_F = 256
        GLOB_F = 64
        HIDDEN = 1024
        N_GRAPHS = 8
        MLP_IN = NODE_F + 3 * EDGE_F + GLOB_F
        col = edge_index[1]
        n = x.shape[0]
        out1 = jax.ops.segment_sum(edge_attr, col, num_segments=n)
        cnt = jax.ops.segment_sum(jnp.ones((edge_attr.shape[0], 1), edge_attr.dtype), col, num_segments=n)
        out2 = jax.ops.segment_max(edge_attr, col, num_segments=n)
        out2 = jnp.where(cnt > 0, out2, jnp.zeros_like(out2))
        out3 = out1 / jnp.maximum(cnt, 1.0)
        h = jnp.concatenate([x, out1, out2, out3, u[batch]], axis=1)
        h = jax.nn.relu(h @ W1 + b1) @ W2 + b2
        return h + x
    edge_index = jnp.stack([src, dst])
    batch0 = jnp.zeros((6250,), jnp.int32)
    h = jnp.maximum(_layernorm(x, axis=-1), 0.0)
    x = x + _L0_gnn_ref(h, edge_attr_96, L0_gnn_u, L0_gnn_W1, L0_gnn_b1, L0_gnn_W2, L0_gnn_b2, edge_index, batch0)
    return x

_drawn_inputs = setup_inputs


def setup_inputs(seed=0):
    import zlib

    import numpy as np

    out = dict(_drawn_inputs(seed))
    spreads = {}
    factors = {'L0_gnn_b1': 8.0, 'L0_gnn_b2': 8.0}
    for name, (base, spread) in spreads.items():
        noise = np.random.default_rng([zlib.crc32(name.encode()), seed]).standard_normal(out[name].shape)
        drawn = base * np.exp(spread * noise) if base else spread * noise
        out[name] = jnp.asarray(drawn.astype(out[name].dtype))
    for name, factor in factors.items():
        out[name] = (out[name] * factor).astype(out[name].dtype)
    return out
```

```python
import itertools

import concourse.bass as bass
from concourse import mybir

P = 128


class Step:

    def __init__(self, const, coef=0, reg=None):
        self.const, self.coef, self.reg = const, coef, reg

    def __add__(self, n):
        return Step(self.const + n, self.coef, self.reg)

    def __sub__(self, n):
        return self + (-n)

    def __mul__(self, n):
        return Step(self.const * n, self.coef * n, self.reg)

    def __floordiv__(self, n):
        assert self.coef % n == 0
        return Step(self.const // n, self.coef // n, self.reg)

    def __mod__(self, n):
        assert self.coef % n == 0
        return self.const % n

    @property
    def value(self):
        return self.const if not self.coef else self.reg * self.coef + self.const


def nth(count):
    if isinstance(count, Step):
        if count.coef:
            assert count.const > 0
            return count.value
        count = count.const
    return max(count, 0)


def gnn_block(nc, x, dst, edge, u, W1, b1, W2, b2, out):
    f32, f32r, i32 = mybir.dt.float32, mybir.dt.float32r, mybir.dt.int32
    ALU, ACT, AX = mybir.AluOpType, mybir.ActivationFunctionType, mybir.AxisListType

    N, D = x.shape
    NE, F = edge.shape
    G = u.shape[1]
    H = W1.shape[1]
    NT = -(-N // P)
    NTP = NT + 1
    BT = 4
    NB = -(-NT // BT)
    HC = H // P
    K = D + 3 * F
    assert K + G == W1.shape[0]
    KC = K // P
    KR = K - KC * P
    CAT = KC * P + 3 * KR
    NJ = 19
    CAPE = NJ * P
    WIN = 16
    XW = 8
    XR = 8
    ROW = 425
    NROW = NE // ROW
    assert NROW * ROW == NE
    LAST = N - (NT - 1) * P
    FMAX = 3.3895e38
    EPS = 1e-5

    sb = {}

    def sbuf(name, shape, dt=f32):
        sb[name] = nc.alloc_sbuf_tensor(name, shape, dt)
        return sb[name]

    w1h, w1l = sbuf("w1h", [P, KC, H], f32r), sbuf("w1l", [P, KC, H], f32r)
    w1r = sbuf("w1r", [3 * KR, H], f32r)
    w2h, w2l = sbuf("w2h", [P, HC, D], f32r), sbuf("w2l", [P, HC, D], f32r)
    b1e, b2b = sbuf("b1e", [P, HC]), sbuf("b2b", [P, D])
    inh = [sbuf(f"inh{i}", [P, KC, BT * P], f32r) for i in range(2)]
    inl = [sbuf(f"inl{i}", [P, KC, BT * P], f32r) for i in range(2)]
    inr = [sbuf(f"inr{i}", [3 * KR, BT * P], f32r) for i in range(2)]
    hf = [sbuf(f"hf{i}", [P, BT * P]) for i in range(2)]
    hh = [sbuf(f"hh{i}", [P, BT * P], f32r) for i in range(4)]
    hl = [sbuf(f"hl{i}", [P, BT * P], f32r) for i in range(4)]
    natn, ohn, elln = NJ * F, NJ * P, 2 * WIN * F
    work = sbuf("work", [P, 2 * (natn + ohn + elln)])
    natf = [work[:, i * natn:(i + 1) * natn] for i in range(2)]
    nat = [t.rearrange("p (j f) -> p j f", f=F) for t in natf]
    ohf = [work[:, 2 * natn + i * ohn:2 * natn + (i + 1) * ohn] for i in range(2)]
    onehot = [t.rearrange("p (j n) -> p j n", n=P) for t in ohf]
    ellf = [work[:, 2 * (natn + ohn) + i * elln:2 * (natn + ohn) + (i + 1) * elln] for i in range(2)]
    ell = [t.rearrange("p (j f) -> p j f", f=F) for t in ellf]
    ndst = [sbuf(f"ndst{i}", [P, NJ], i32) for i in range(4)]
    dloc = sbuf("dloc", [P, NJ])
    mx = sbuf("mx", [P, 2, F])
    mx2 = sbuf("mx2", [P, F])
    mxx = sbuf("mxx", [P, F])
    cat = [sbuf(f"cat{i}", [P, CAT]) for i in range(2)]
    xin = [sbuf(f"xin{i}", [P, D]) for i in range(2)]
    xball = sbuf("xb", [P, 8 * D])
    xb = [xball[:, i * D:(i + 1) * D] for i in range(8)]
    yc = sbuf("yc", [P, 4, D])
    yo = sbuf("yo", [P, 4, D])
    M_MASK, M_BOUND, M_ANY, M_RCNT, M_BASE, M_RSTD, M_OFF, M_S, M_E8, NM = 0, 16, 17, 18, 19, 20, 21, 22, 23, 24
    tab = sbuf("tab", [P, NTP, NM])
    tabi = sbuf("tabi", [P, NTP, 2], i32)
    stg = [sbuf(f"stg{i}", [P, NM]) for i in range(4)]
    stgi = [sbuf(f"stgi{i}", [P, 2], i32) for i in range(4)]
    ident = sbuf("ident", [P, P])
    iota = sbuf("iota", [P, P])
    e0row = sbuf("e0row", [1, NTP], i32)
    rawf = ohf
    scratch = sbuf("scratch", [P, 20 * NTP])
    cols = [scratch[:, i * NTP:(i + 1) * NTP] for i in range(20)]
    nid, cnt1, cnt2, rowi = cols[0], cols[1], cols[2], cols[3].bitcast(i32)
    rows = [natf[1][:, i * ROW:(i + 1) * ROW].bitcast(i32) for i in range(4)]
    hfw = [yc[:, :, :], yo[:, :, :]]
    small = cols[4:13]
    Dg = small[4]
    stats = scratch[:, 13 * NTP:13 * NTP + 6 * NT].rearrange("p (t s) -> p t s", s=6)
    mv = sbuf("mv", [P, NTP, 2])
    pid = sbuf("pid", [P, 1])
    shift = sbuf("shift", [NTP, NTP])
    ones = sbuf("ones", [1, P])
    fi = yo[0:1, 0, 0:NROW].bitcast(i32)
    ff = yo[0:1, 1, 0:NROW]
    trisb = sbuf("tri", [NTP, NTP])
    rcum = sbuf("rcum", [1, 2, NTP], i32)
    flag = sbuf("flag", [1, 1], i32)
    onesc = sbuf("onesc", [P, 1])
    bad = sbuf("bad", [P, 2])
    dm = sbuf("dm", [NTP, 8])
    xi, xif = sbuf("xi", [P, 1], i32), sbuf("xif", [P, 2])
    xw = scratch[:, 0:XW * F]
    gst = sbuf("gst", [P, 2, F])
    sumT, maxT = work[:, 0:NT * P], work[:, NT * P:2 * NT * P]
    eT = work[:, 2 * NT * P:2 * NT * P + ROW]
    gdst = work[0:1, 2 * NT * P + ROW:2 * NT * P + 2 * ROW].bitcast(i32)
    fb = hf[1][:, 0:NROW]
    et, st = sbuf("et", [NTP, P]), sbuf("st", [NTP, P])
    m16 = [t.rearrange("p (t w) -> p t w", w=WIN) for t in
           (natf[0][:, H:H + NTP * WIN], ellf[1][:, 7 * D:7 * D + NTP * WIN])]
    iota16 = sbuf("iota16", [P, WIN])
    u0 = sbuf("u0", [G, 1])
    w1u = ellf[0][0:G, 7 * D:7 * D + H]
    b1c = sbuf("b1c", [P, HC])
    junk = [ellf[1][:, 7 * D + NTP * WIN:7 * D + NTP * WIN + ROW], hf[0][:, 0:ROW]]

    def psum(name, shape):
        return nc.alloc_psum_tensor(name, shape, f32)

    l1ps = [psum(f"l1ps{i}", [P, BT * P]) for i in range(2)]
    yps = [psum(f"yps{i}", [P, 2 * D]) for i in range(2)]
    tps, tpr = psum("tps", [P, BT * P]), psum("tpr", [P, BT * P])
    sps = [psum(f"sps{i}", [P, 512]) for i in range(2)]

    S = nc.alloc_semaphore
    w_in, r_in, w2_in, c_in = S("w_in"), S("r_in"), S("w2_in"), S("c_in")
    consts, f_in, f_row, f_ps, f_sb = S("consts"), S("f_in"), S("f_row"), S("f_ps"), S("f_sb")
    cnt1_done, row_done, rowbuf_used = S("cnt1_done"), S("row_done"), S("rowbuf_used")
    rowbuf_in = [S(f"rows_or_stores{i}") for i in range(4)]
    dve_set, pe_set, act_set, pool_set = S("dve_set"), S("pe_set"), S("act_set"), S("pool_set")
    xs_in = [S(f"xs_in{i}") for i in range(2)]
    xs_used, e0_ready, setup_free = S("xs_used"), S("e0_ready"), S("setup_free")
    var_ready, std_ready = S("var_ready"), S("std_ready")
    ends_ready, et_ready, st_ready, dcol_ready = S("ends_ready"), S("et_ready"), S("st_ready"), S("dcol_ready")
    nat_in = [S(f"nat_in{i}") for i in range(2)]
    ndst_in = [S(f"ndst_in{i}") for i in range(4)]
    x_in = [S(f"x_in{i}") for i in range(2)]
    ell_in = [S(f"ell_in{i}") for i in range(2)]
    dloc_done, oh_done, sums_done, trans_done = S("dloc_done"), S("oh_done"), S("sums_done"), S("trans_done")
    l1_done, l2_done = S("l1_done"), S("l2_done")
    hi_done, lo_done, hiT_done, loT_done = S("hi_done"), S("lo_done"), S("hiT_done"), S("loT_done")
    h_done, outs_done, masked, maxes, max2, out2_done = (S(n) for n in
        ("h_done", "outs_done", "masked", "maxes", "max2", "out2_done"))
    stg_done, xb_part, xb_done, add_done, evac_done = (S(n) for n in
        ("stg_done", "xb_part", "xb_done", "add_done", "evac_done"))
    gmix, dve_turn = S("gmix"), S("dve_turn")
    pool_turn, sd_in, x_idx, x_in_w, x_red, x_used = (S(n) for n in ("pool_turn", "sd_in", "x_idx", "x_in_w", "x_red", "x_used"))
    flag_ready, g_in, g_used, g_upd, g_done, g_out, gc_in, gt_in, gt_used = (S(n) for n in
        ("flag_ready", "g_in", "g_used", "g_upd", "g_done", "g_out", "gc_in", "gt_in", "gt_used"))
    stored = rowbuf_in
    gathered = [16 * len(range(r, NTP, 4)) for r in range(4)]

    edge_rows = edge
    gsum = nc.dram_tensor("gsum", [NT * P, F], f32, kind="Internal").ap()
    gmax = nc.dram_tensor("gmax", [NT * P, F], f32, kind="Internal").ap()
    gcnt = nc.dram_tensor("gcnt", [1, NT * P], f32, kind="Internal").ap()
    dst_row = dst.rearrange("(r c) -> r c", c=ROW)

    SC = 2 * ROW
    SR = NE // SC
    assert SR * SC == NE and SR <= P and SC < 4 * D
    sd = xball[:, 0:SC + 1].bitcast(i32)
    sbad = xball[:, 4 * D:4 * D + SC]

    XG = 7
    XGF = NT // XG
    assert XGF * XG == NT
    xs = [ellf[i][:, 0:XG * D].rearrange("p (t d) -> p t d", d=D) for i in range(2)]

    def steps(eng, body):
        for t in range(-2, 8):
            body(Step(t))
        with eng.Fori(0, 5) as i:
            for t in range(8, 16):
                body(Step(t, 8, i))
        for t in range(48, 57):
            body(Step(t))

    def is_tile(T, n=NT):
        return bool(T.coef) or 0 <= T.const < n

    def is_chunk(C):
        return bool(C.coef) or 0 <= C.const < NC_ALL

    NC_ALL = HC * NB

    def columns(C):
        return P if (not C.coef and C.const // HC == NB - 1) else BT * P

    with nc.Block() as block:

        @block.sync
        def _(sp):
            sp.dma_start(fi, dst_row[:, 0:1].rearrange("r c -> c r"), allow_slow_non_contiguous=True).then_inc(f_in, 16)
            def load_x(g):
                sp.wait_ge(xs_used, nth((g - 1) * XG))
                full = XG if g < XGF - 1 else XG - 1
                sp.dma_start(xs[g % 2][:, 0:full, :],
                             x[g * XG * P:(g * XG + full) * P, :].rearrange("(t p) d -> p t d", p=P)).then_inc(xs_in[g % 2], 16)
                if full < XG:
                    sp.dma_start(xs[g % 2][0:LAST, full, :], x[(NT - 1) * P:N, :]).then_inc(xs_in[g % 2], 16)
            sp.dma_start(sd[0:SR, 0:SC], dst.rearrange("(r c) -> r c", c=SC)).then_inc(sd_in, 16)
            sp.wait_ge(consts, 9)
            sp.dma_start(sd[0:SR - 1, SC:SC + 1], dst.rearrange("(r c) -> r c", c=SC)[1:SR, 0:1], allow_slow_non_contiguous=True).then_inc(sd_in, 16)
            load_x(0)
            load_x(1)
            for c in range(0, KC, 2):
                sp.dma_start(rawf[c // 2][:, 0:2 * H].rearrange("p (c h) -> p c h", h=H),
                             W1[c * P:(c + 2) * P, :].rearrange("(c p) h -> p c h", p=P)).then_inc(w_in, 16)
            for r in range(3):
                sp.dma_start(natf[0][r * KR:(r + 1) * KR, 0:H], W1[KC * P:K, :]).then_inc(r_in, 16)
            sp.wait_ge(f_ps, 1)
            for c in range(2):
                sp.dma_start(hfw[c], W2[c * 4 * P:(c + 1) * 4 * P, :].rearrange("(c p) d -> p c d", p=P)).then_inc(w2_in, 16)
            sp.dma_start(w1u, W1[K:K + G, :]).then_inc(c_in, 16)
            sp.dma_start(u0[:, :], u[0:1, :].rearrange("a g -> g a"), allow_slow_non_contiguous=True).then_inc(c_in, 16)
            sp.dma_start(b1c[:, :], b1.rearrange("(c p) -> p c", p=P), allow_slow_non_contiguous=True).then_inc(c_in, 16)
            sp.dma_start(b2b[:, :], b2.rearrange("(a d) -> a d", a=1).broadcast_to([P, D])).then_inc(c_in, 16)
            for g in range(2, XGF):
                load_x(g)
            sp.wait_ge(e0_ready, 1)
            sp.wait_ge(setup_free, 1)
            sp.wait_ge(flag_ready, 1)
            general = sp.value_load(flag[0:1, 0:1], min_val=0, max_val=1)
            with sp.If(general > 0):
                with sp.Fori(0, NROW) as r:
                    sp.wait_ge(g_used, r + 1)
                    sp.dma_start(gdst, dst_row[bass.ds(r, 1), :]).then_inc(g_in, 16)
                    sp.dma_start(eT[0:F, :], edge[bass.ds(r * ROW, ROW), :].rearrange("e f -> f e"), allow_slow_non_contiguous=True).then_inc(g_in, 16)
                sp.wait_ge(g_done, 1)
                sp.dma_start(gsum.rearrange("n f -> f n"), sumT[0:F, :], allow_slow_non_contiguous=True).then_inc(g_out, 16)
                sp.dma_start(gmax.rearrange("n f -> f n"), maxT[0:F, :], allow_slow_non_contiguous=True).then_inc(g_out, 16)
                sp.dma_start(gcnt, sumT[F:F + 1, :]).then_inc(g_out, 16)
                sp.wait_ge(g_out, 48)
                sp.dma_start(tab[:, 0:NT - 1, M_ANY], gcnt[0:1, 0:(NT - 1) * P].rearrange("a (t p) -> (a p) t", p=P), allow_slow_non_contiguous=True).then_inc(gc_in, 16)
                sp.dma_start(tab[0:LAST, NT - 1:NT, M_ANY], gcnt[0:1, (NT - 1) * P:N].rearrange("a (t p) -> (a p) t", t=1), allow_slow_non_contiguous=True).then_inc(gc_in, 16)
            sp.wait_ge(setup_free, 2)

            def body(T):
                D2 = T + 2
                if is_tile(D2, NTP):
                    sp.wait_ge(dloc_done, nth(D2 - 3))
                    first = sp.value_load(e0row[0:1, bass.ds(D2.value, 1)], min_val=0, max_val=NE - CAPE)
                    sp.dma_start(ndst[D2 % 4][:, :], dst[bass.ds(first, CAPE)].rearrange("(p j) -> p j", j=NJ)).then_inc(ndst_in[D2 % 4], 16)
                G = T + 1
                if is_tile(G):
                    with sp.If(general > 0):
                        sp.wait_ge(gt_used, nth(G))
                        n = P if (G.coef or G.const < NT - 1) else LAST
                        at = bass.ds(G.value * P, P) if G.coef else slice(G.const * P, G.const * P + n)
                        sp.dma_start(gst[0:n, 0, :], gsum[at, :]).then_inc(gt_in, 16)
                        sp.dma_start(gst[0:n, 1, :], gmax[at, :]).then_inc(gt_in, 16)
                if is_tile(T):
                    first = sp.value_load(e0row[0:1, bass.ds(T.value, 1)], min_val=0, max_val=NE - CAPE)
                    sp.wait_ge(sums_done, nth(T - 1))
                    sp.dma_start(nat[T % 2][:, :, :], edge_rows[bass.ds(first, CAPE), :].rearrange("(p j) f -> p j f", j=NJ)).then_inc(nat_in[T % 2], 16)
                    sp.wait_ge(xb_done, nth(T - 1))
                    sp.wait_ge(h_done, nth(T - 1))
                    if T.coef or T.const < NT - 1:
                        sp.dma_start(xin[T % 2][:, :], x[bass.ds(T.value * P, P), :] if T.coef else x[T.const * P:(T.const + 1) * P, :]).then_inc(x_in[T % 2], 16)
                    else:
                        sp.dma_start(xin[T % 2][0:LAST, :], x[T.const * P:N, :]).then_inc(x_in[T % 2], 16)
            steps(sp, body)

        @block.gpsimd
        def _(pool):
            kw = dict(allow_small_or_imprecise_dtypes=True)
            pool.sem_inc(add_done, 1)
            pool.iota(iota[:, :], pattern=[[1, P]], base=0, channel_multiplier=0, **kw).then_inc(consts, 1)
            pool.iota(pid[:, :], pattern=[[1, 1]], base=0, channel_multiplier=1, **kw).then_inc(consts, 1)
            pool.iota(nid[:, :], pattern=[[P, NTP]], base=0, channel_multiplier=1, **kw).then_inc(consts, 1)
            pool.iota(iota16[:, :], pattern=[[1, WIN]], base=0, channel_multiplier=0, **kw).then_inc(consts, 1)
            pool.iota(tab[:, :, M_BASE], pattern=[[P, NTP]], base=0, channel_multiplier=0, **kw).then_inc(consts, 1)
            pool.memset(ones[:, :], 1.0).then_inc(consts, 1)
            pool.memset(sd[:, SC:SC + 1], N).then_inc(consts, 1)
            pool.memset(onesc[:, :], 1.0).then_inc(consts, 1)
            pool.memset(bad[:, :], 0.0).then_inc(consts, 1)
            for t in range(NTP):
                pool.wait_ge(row_done, nth(t // 10 + 1 if t % 10 == 0 else 0))
                pool.wait_ge(rowbuf_used, nth(t - 3))
                pool.indirect_dma_start(out=rows[t % 4], out_offset=None, in_=dst_row,
                                        in_offset=bass.IndirectOffsetOnAxis(ap=rowi[:, t:t + 1], axis=0)).then_inc(rowbuf_in[t % 4], 16)

            pool.wait_ge(setup_free, 2)

            def body(T):
                A = T + 2
                if is_tile(A, NTP):
                    pool.wait_ge(outs_done, nth(A - 3))
                    pool.wait_ge(out2_done, nth(A - 3))
                    pool.wait_ge(maxes, nth((A - 1) * 2))
                    pool.sem_inc(pool_turn, 1)
                    at = A.value
                    pool.tensor_copy(stg[A % 4][:, :], tab[:, bass.ds(at, 1), :]).then_inc(stg_done, 1)
                    pool.tensor_copy(stgi[A % 4][:, :], tabi[:, bass.ds(at, 1), :]).then_inc(stg_done, 1)
                    pool.wait_ge(stg_done, nth(A * 2 + 2))
                    pool.sem_inc(pool_turn, 1)
                    for w in range(2):
                        pool.indirect_dma_start(out=ellf[A % 2][:, w * WIN * F:(w + 1) * WIN * F], out_offset=None, in_=edge,
                                                in_offset=bass.IndirectOffsetOnAxis(ap=stgi[A % 4][:, w:w + 1], axis=0)).then_inc(ell_in[A % 2], 16)
                    rounds = pool.value_load(rcum[0:1, 0, bass.ds(at, 1)], min_val=0, max_val=XR)
                    before = pool.value_load(rcum[0:1, 1, bass.ds(at, 1)], min_val=0, max_val=XR * NTP)
                    with pool.If(rounds > 0):
                        g = stg[A % 4]
                        pool.tensor_scalar(out=xif[:, 0:1], in0=g[:, M_S:M_S + 1], scalar1=float(WIN - XW), scalar2=None, op0=ALU.add).then_inc(pool_turn, 1)
                        with pool.Fori(0, rounds) as q:
                            pool.wait_ge(x_used, before + q + 1)
                            pool.sem_inc(pool_turn, 1)
                            pool.drain()
                            pool.tensor_scalar(out=xif[:, 0:1], in0=xif[:, 0:1], scalar1=float(XW), scalar2=None, op0=ALU.add).then_inc(x_idx, 1)
                            pool.wait_ge(x_idx, (before + q) * 3 + 1)
                            pool.sem_inc(pool_turn, 1)
                            pool.tensor_scalar(out=xif[:, 1:2], in0=xif[:, 0:1], scalar1=g[:, M_E8:M_E8 + 1], scalar2=g[:, M_S:M_S + 1], op0=ALU.min, op1=ALU.max).then_inc(x_idx, 1)
                            pool.wait_ge(x_idx, (before + q) * 3 + 2)
                            pool.sem_inc(pool_turn, 1)
                            pool.tensor_scalar(out=xi[:, :], in0=xif[:, 1:2], scalar1=float(NE - XW), scalar2=None, op0=ALU.min).then_inc(x_idx, 1)
                            pool.wait_ge(x_idx, (before + q) * 3 + 3)
                            pool.sem_inc(pool_turn, 1)
                            pool.indirect_dma_start(out=xw, out_offset=None, in_=edge,
                                                    in_offset=bass.IndirectOffsetOnAxis(ap=xi[:, 0:1], axis=0)).then_inc(x_in_w, 16)
                U = T - 8
                if is_tile(U):
                    rows_ = P if (U.coef or U.const < NT - 1) else LAST
                    pool.wait_ge(evac_done, nth(U + 1))
                    pool.wait_ge(stored[U % 4], nth((U // 4) * 16 + gathered[U % 4]))
                    pool.tensor_tensor(out=yo[:, U % 4, :], in0=yc[:, U % 4, :], in1=xb[U % 8][:, :], op=ALU.add).then_inc(add_done, 1)
                    pool.wait_ge(add_done, nth(U + 2))
                    pool.sem_inc(pool_turn, 1)
                    where = out[bass.ds(U.value * P, P), :] if U.coef else out[U.const * P:U.const * P + rows_, :]
                    pool.dma_start(where, yo[0:rows_, U % 4, :]).then_inc(stored[U % 4], 16)
                if is_tile(T):
                    pool.wait_ge(h_done, nth(T + 1))
                    pool.wait_ge(xb_part, nth(T))
                    pool.wait_ge(add_done, nth(T - 6))
                    pool.tensor_tensor(out=xb[T % 8][:, :], in0=xin[T % 2][:, :], in1=cat[T % 2][:, 0:D], op=ALU.add).then_inc(xb_part, 1)
                    pool.wait_ge(xb_part, nth(T + 1))
                    pool.tensor_tensor(out=xb[T % 8][:, :], in0=xb[T % 8][:, :], in1=b2b[:, :], op=ALU.add).then_inc(xb_done, 1)
            pool.wait_ge(c_in, 64)
            steps(pool, body)
            for r in range(4):
                pool.wait_ge(stored[r], nth(16 * len(range(r, NT, 4)) + gathered[r]))
            for r in range(2):
                pool.wait_ge(ell_in[r], nth(32 * len(range(r, NTP, 2))))

        @block.scalar
        def _(act):
            n = 0
            for c in range(0, KC, 2):
                act.wait_ge(w_in, 8 * KC)
                act.activation(w1h[:, c:c + 2, :], rawf[c // 2][:, 0:2 * H].rearrange("p (c h) -> p c h", h=H), ACT.Copy).then_inc(act_set, 1)
            act.wait_ge(r_in, 48)
            act.activation(w1r[:, :], natf[0][0:3 * KR, 0:H], ACT.Copy).then_inc(act_set, 1)
            act.wait_ge(w2_in, 32)
            for c in range(2):
                act.activation(w2h[:, c * 4:(c + 1) * 4, :], hfw[c], ACT.Copy).then_inc(act_set, 1)
            act.wait_ge(var_ready, 1)
            act.activation(small[7][:, 0:NT], small[8][:, 0:NT], ACT.Sqrt).then_inc(std_ready, 1)
            act.wait_ge(setup_free, 2)

            def relu(C):
                cols = columns(C)
                m = C % HC
                act.wait_ge(l1_done, nth(C + 1))
                act.wait_ge(lo_done, nth(C - 1))
                act.activation(hf[C % 2][:, 0:cols], l1ps[C % 2][:, 0:cols], ACT.Relu, bias=b1e[:, m:m + 1]).then_inc(hi_done, 1)
                act.wait_ge(l2_done, nth(C - 3))
                act.activation(hh[C % 4][:, 0:cols], l1ps[C % 2][:, 0:cols], ACT.Relu, bias=b1e[:, m:m + 1]).then_inc(hi_done, 1)

            def body(T):
                C = (T - 4) * 2
                if is_chunk(C):
                    relu(C)
                if is_tile(T):
                    b, k = (T // 4) % 2, T % 4
                    act.wait_ge(trans_done, nth(T + 1))
                    act.activation(inh[b][:, :, k * P:(k + 1) * P], tps[:, :].rearrange("p (c n) -> p c n", n=P), ACT.Copy).then_inc(hiT_done, 1)
                    act.activation(inr[b][:, k * P:(k + 1) * P], tpr[0:3 * KR, 0:P], ACT.Copy).then_inc(hiT_done, 1)
                A = T + 1
                if is_tile(A):
                    act.wait_ge(x_in[A % 2], nth((A // 2) * 16 + 16))
                    act.wait_ge(stg_done, nth(A * 2 + 2))
                    act.wait_ge(trans_done, nth(A - 1))
                    act.wait_ge(xb_done, nth(A - 1))
                    act.activation(cat[A % 2][:, 0:D], xin[A % 2][:, :], ACT.Relu, bias=stg[A % 4][:, M_OFF:M_OFF + 1],
                                   scale=stg[A % 4][:, M_RSTD:M_RSTD + 1]).then_inc(h_done, 1)
                if T % 4 == 0 and is_chunk(C - HC):
                    first = T - 8
                    act.wait_ge(l2_done, nth((T // 4 - 1) * HC))
                    act.wait_ge(add_done, nth(first + 1))
                    for j in range(BT if (T.coef or T.const < 56) else 1):
                        act.activation(yc[:, j, :], yps[j // 2][:, (j % 2) * D:(j % 2 + 1) * D], ACT.Copy).then_inc(evac_done, 1)
                if is_chunk(C + 1):
                    relu(C + 1)
                if is_tile(A):
                    q = sps[A % 2]
                    c, s = cat[A % 2], stg[A % 4]
                    act.wait_ge(sums_done, nth(A + 1))
                    act.activation(c[:, D:D + F], q[:, 0:F], ACT.Copy)
                    act.activation(c[:, D + 2 * F:KC * P], q[:, 0:F - KR], ACT.Copy, scale=s[:, M_RCNT:M_RCNT + 1])
                    act.activation(c[:, KC * P:CAT].rearrange("p (r k) -> p r k", k=KR), q[:, None, F - KR:F].broadcast_to([P, 3, KR]),
                                   ACT.Copy, scale=s[:, M_RCNT:M_RCNT + 1]).then_inc(outs_done, 1)
            steps(act, body)

        @block.tensor
        def _(pe):
            pe.wait_ge(f_row, 1)
            pe.wait_ge(consts, 9)
            pe.matmul(tps[:, 0:NROW], ones[0:1, :], ff, start=True, stop=True).then_inc(f_ps, 1)
            pe.wait_ge(ends_ready, 1)
            pe.transpose(sps[0][0:NTP, 0:P], small[0][:, 0:NTP], ident[:, :]).then_inc(pe_set, 1)
            pe.wait_ge(et_ready, 1)
            pe.matmul(sps[1][0:NTP, 0:1], shift[:, :], et[:, P - 1:P], start=True, stop=True).then_inc(pe_set, 1)
            pe.matmul(l1ps[0][0:1, 0:NTP], et[:, P - 1:P], shift[:, :], start=True, stop=True).then_inc(pe_set, 1)
            pe.wait_ge(st_ready, 1)
            pe.transpose(l1ps[1][:, 0:NTP], st[:, :], ident[0:NTP, 0:NTP]).then_inc(pe_set, 1)
            pe.wait_ge(dcol_ready, 1)
            pe.transpose(sps[0][0:NTP, 0:P], Dg[:, :], ident[:, :]).then_inc(pe_set, 1)
            pe.wait_ge(dcol_ready, 2)
            pe.matmul(l1ps[0][0:1, 0:NTP], dm[:, 1:2], ident[0:NTP, 0:NTP], start=True, stop=True)
            pe.matmul(sps[1][0:1, 0:NTP], dm[:, 1:2], trisb[:, :], start=True, stop=True)
            pe.matmul(sps[0][0:1, 0:2], onesc[:, :], bad[:, :], start=True, stop=True).then_inc(pe_set, 1)
            pe.wait_ge(c_in, 64)
            for m in range(HC):
                last = pe.matmul(tpr[:, m:m + 1], w1u[:, m * P:(m + 1) * P], u0[:, :], start=True, stop=True)
            last.then_inc(pe_set, 1)
            pe.wait_ge(setup_free, 2)

            def layer1(C):
                b, m, cols = (C // HC) % 2, C % HC, columns(C)
                pe.wait_ge(hi_done, nth((C - 1) * 2))
                first = True
                ms = slice(m * P, (m + 1) * P)
                for c in range(KC):
                    for wt, it in ((w1h, inh), (w1l, inh), (w1h, inl)):
                        pe.matmul(l1ps[C % 2][:, 0:cols], wt[:, c, ms], it[b][:, c, 0:cols], start=first, stop=False)
                        first = False
                pe.matmul(l1ps[C % 2][:, 0:cols], w1r[:, ms], inr[b][:, 0:cols], start=False, stop=True).then_inc(l1_done, 1)

            def layer2(C):
                m, cols = C % HC, columns(C)
                pe.wait_ge(lo_done, nth(C + 1))
                if m == 0:
                    pe.wait_ge(evac_done, nth((C // HC) * 4))
                for j in range(cols // P):
                    for ht, wt in ((hh, w2h), (hh, w2l), (hl, w2h)):
                        last = pe.matmul(yps[j // 2][:, (j % 2) * D:(j % 2 + 1) * D], ht[C % 4][:, j * P:(j + 1) * P], wt[:, m, :],
                                         start=(m == 0 and j % 2 == 0 and ht is hh and wt is w2h), stop=(m == HC - 1 and ht is hl),
                                         skip_group_check=True)
                last.then_inc(l2_done, 1)

            def body(T):
                C = (T - 4) * 2
                if is_chunk(C - 2):
                    layer2(C - 2)
                if is_chunk(C):
                    if C % HC == 0:
                        n = T if (T.coef or T.const < 52) else Step(NT)
                        pe.wait_ge(loT_done, nth(n))
                    layer1(C)
                if is_tile(T):
                    pe.wait_ge(out2_done, nth(T + 1))
                    pe.wait_ge(outs_done, nth(T + 1))
                    pe.wait_ge(loT_done, nth(T))
                    for c in range(KC):
                        pe.transpose(tps[:, c * P:(c + 1) * P], cat[T % 2][:, c * P:(c + 1) * P], ident[:, :])
                    pe.transpose(tpr[0:3 * KR, 0:P], cat[T % 2][:, KC * P:CAT], ident[:, :]).then_inc(trans_done, 1)
                if is_chunk(C - 1):
                    layer2(C - 1)
                if is_chunk(C + 1):
                    layer1(C + 1)
                A = T + 1
                if is_tile(A):
                    pe.wait_ge(oh_done, nth(A + 1))
                    pe.wait_ge(nat_in[A % 2], nth((A // 2) * 16 + 16))
                    pe.wait_ge(outs_done, nth(A - 1))
                    for j in range(NJ):
                        last = pe.matmul(sps[A % 2][:, 0:F], onehot[A % 2][:, j, :], nat[A % 2][:, j, :], start=(j == 0), stop=(j == NJ - 1))
                    last.then_inc(sums_done, 1)
            steps(pe, body)

        @block.vector
        def _(dve):
            set_step = itertools.count(1)
            V = dve
            V.sem_inc(x_used, 1)
            V.sem_inc(g_used, 1)
            dve.wait_ge(consts, 9)
            V.tensor_scalar(out=ident[:, :], in0=iota[:, :], scalar1=pid[:, 0:1], scalar2=None, op0=ALU.is_equal).then_inc(dve_set, 1)
            dve.wait_ge(dve_set, next(set_step))
            V.tensor_scalar(out=small[1][:, 0:1], in0=pid[:, :], scalar1=1.0, scalar2=None, op0=ALU.add).then_inc(dve_set, 1)
            dve.wait_ge(dve_set, next(set_step))
            V.tensor_scalar(out=trisb[:, :], in0=iota[0:NTP, 0:NTP], scalar1=pid[0:NTP, 0:1], scalar2=None, op0=ALU.is_gt).then_inc(dve_set, 1)
            dve.wait_ge(dve_set, next(set_step))
            V.tensor_scalar(out=shift[:, :], in0=iota[0:NTP, 0:NTP], scalar1=small[1][0:NTP, 0:1], scalar2=None, op0=ALU.is_equal).then_inc(dve_set, 1)
            dve.wait_ge(dve_set, next(set_step))
            dve.wait_ge(f_in, 16)
            V.tensor_copy(ff, fi).then_inc(f_row, 1)
            dve.wait_ge(f_ps, 1)
            V.tensor_copy(fb, tps[:, 0:NROW]).then_inc(dve_set, 1)
            dve.wait_ge(dve_set, next(set_step))
            for t in range(NTP):
                dve.wait_ge(cnt1_done, nth(t - 1))
                V.tensor_scalar(out=junk[t % 2][:, 0:NROW], in0=fb, scalar1=nid[:, t:t + 1], scalar2=0.0, op0=ALU.is_le, op1=ALU.add,
                                accum_out=cnt1[:, t:t + 1]).then_inc(cnt1_done, 1)
                if t % 10 == 9 or t == NTP - 1:
                    g = slice(t - t % 10, t + 1)
                    dve.wait_ge(cnt1_done, nth(t + 1))
                    V.tensor_scalar(out=small[2][:, g], in0=cnt1[:, g], scalar1=1.0, scalar2=-1.0, op0=ALU.max, op1=ALU.add).then_inc(dve_set, 1)
                    dve.wait_ge(dve_set, next(set_step))
                    V.tensor_copy(rowi[:, g], small[2][:, g]).then_inc(row_done, 1)
            def stats_of(t):
                g = t // XG
                if t % XG == 0:
                    dve.wait_ge(xs_in[g % 2], nth(16 * (g // 2 + 1) + (16 if g == XGF - 1 else 0)))
                V.bn_stats(out=stats[:, t, :], in_=xs[g % 2][:, t % XG, :]).then_inc(xs_used, 1)
                dve.wait_ge(xs_used, nth(t + 1))
                V.bn_aggr(out=mv[:, t, :], in_=stats[:, t, :]).then_inc(dve_set, 1)
                dve.wait_ge(dve_set, next(set_step))
            for t in range(NTP):
                dve.wait_ge(rowbuf_in[t % 4], nth(16 * (t // 4 + 1)))
                dve.wait_ge(rowbuf_used, nth(t - 1))
                V.tensor_scalar(out=junk[t % 2], in0=rows[t % 4], scalar1=nid[:, t:t + 1], scalar2=0.0, op0=ALU.is_le, op1=ALU.add,
                                accum_out=cnt2[:, t:t + 1]).then_inc(rowbuf_used, 1)
                if t < NT:
                    stats_of(t)
            dve.wait_ge(rowbuf_used, NTP)
            V.scalar_tensor_tensor(out=small[0][:, :], in0=small[2][:, :], scalar=float(ROW), in1=cnt2[:, :], op0=ALU.mult, op1=ALU.add).then_inc(ends_ready, 1)
            dve.wait_ge(pe_set, 1)
            V.tensor_copy(et[:, :], sps[0][0:NTP, 0:P]).then_inc(et_ready, 1)
            dve.wait_ge(et_ready, 1)
            V.tensor_copy(st[:, 1:P], et[:, 0:P - 1]).then_inc(dve_set, 1)
            dve.wait_ge(dve_set, next(set_step))
            dve.wait_ge(pe_set, 3)
            V.tensor_copy(st[:, 0:1], sps[1][0:NTP, 0:1]).then_inc(st_ready, 1)
            V.tensor_scalar(out=small[1][0:1, :], in0=l1ps[0][0:1, 0:NTP], scalar1=float(NE - CAPE), scalar2=None, op0=ALU.min).then_inc(dve_set, 1)
            dve.wait_ge(dve_set, next(set_step))
            V.tensor_copy(e0row[:, :], small[1][0:1, :]).then_inc(e0_ready, 1)
            dve.wait_ge(pe_set, 4)
            E, B = small[0], small[3]
            V.tensor_copy(B[:, :], l1ps[1][:, 0:NTP]).then_inc(dve_set, 1)
            dve.wait_ge(dve_set, next(set_step))
            V.tensor_tensor(out=Dg[:, :], in0=E[:, :], in1=B[:, :], op=ALU.subtract).then_inc(dcol_ready, 1)
            dve.wait_ge(dcol_ready, 1)
            dve.wait_ge(pe_set, 5)
            V.tensor_reduce(out=dm[:, 0:1], in_=sps[0][0:NTP, 0:P], axis=AX.X, op=ALU.max).then_inc(dve_set, 1)
            dve.wait_ge(dve_set, next(set_step))
            V.memset(dm[:, 1:2], 0.0).then_inc(dve_set, 1)
            dve.wait_ge(dve_set, next(set_step))
            for q in range(XR):
                V.scalar_tensor_tensor(out=dm[:, 1:2], in0=dm[:, 0:1], scalar=float(2 * WIN + q * XW), in1=dm[:, 1:2], op0=ALU.is_gt, op1=ALU.add).then_inc(dve_set, 1)
                dve.wait_ge(dve_set, next(set_step))
            V.tensor_scalar(out=dm[:, 2:3], in0=st[:, 0:1], scalar1=float(NE - CAPE), scalar2=float(CAPE), op0=ALU.min, op1=ALU.add).then_inc(dve_set, 1)
            dve.wait_ge(dve_set, next(set_step))
            V.tensor_tensor(out=dm[:, 3:4], in0=et[:, P - 1:P], in1=dm[:, 2:3], op=ALU.is_gt).then_inc(dve_set, 1)
            dve.wait_ge(dve_set, next(set_step))
            V.scalar_tensor_tensor(out=bad[0:NTP, 0:1], in0=dm[:, 0:1], scalar=float(2 * WIN + XR * XW), in1=dm[:, 3:4], op0=ALU.is_gt, op1=ALU.add).then_inc(dve_set, 1)
            dve.wait_ge(dve_set, next(set_step))
            dve.wait_ge(sd_in, 32)
            V.tensor_tensor(out=sbad[0:SR, :], in0=sd[0:SR, 0:SC], in1=sd[0:SR, 1:SC + 1], op=ALU.is_gt).then_inc(dve_set, 1)
            dve.wait_ge(dve_set, next(set_step))
            V.tensor_reduce(out=bad[0:SR, 1:2], in_=sbad[0:SR, :], axis=AX.X, op=ALU.max).then_inc(dcol_ready, 1)
            dve.wait_ge(pe_set, 6)
            V.tensor_copy(rcum[:, 0, :], l1ps[0][0:1, 0:NTP]).then_inc(dve_set, 1)
            dve.wait_ge(dve_set, next(set_step))
            V.tensor_copy(rcum[:, 1, :], sps[1][0:1, 0:NTP]).then_inc(dve_set, 1)
            dve.wait_ge(dve_set, next(set_step))
            V.tensor_copy(bad[0:1, :], sps[0][0:1, 0:2]).then_inc(dve_set, 1)
            dve.wait_ge(dve_set, next(set_step))
            V.tensor_tensor(out=bad[0:1, 0:1], in0=bad[0:1, 0:1], in1=bad[0:1, 1:2], op=ALU.add).then_inc(dve_set, 1)
            dve.wait_ge(dve_set, next(set_step))
            V.tensor_scalar(out=flag[:, :], in0=bad[0:1, 0:1], scalar1=0.5, scalar2=None, op0=ALU.is_gt).then_inc(flag_ready, 1)
            V.tensor_copy(tab[:, :, M_S], B[:, :]).then_inc(dve_set, 1)
            dve.wait_ge(dve_set, next(set_step))
            V.tensor_scalar(out=tab[:, :, M_E8], in0=E[:, :], scalar1=float(-XW), scalar2=None, op0=ALU.add).then_inc(dve_set, 1)
            dve.wait_ge(dve_set, next(set_step))
            V.tensor_scalar(out=tab[:, :, M_ANY], in0=Dg[:, :], scalar1=1.0, scalar2=None, op0=ALU.min).then_inc(dve_set, 1)
            dve.wait_ge(dve_set, next(set_step))
            V.tensor_scalar(out=small[5][:, :], in0=Dg[:, :], scalar1=1.0, scalar2=None, op0=ALU.max).then_inc(dve_set, 1)
            dve.wait_ge(dve_set, next(set_step))
            V.reciprocal(tab[:, :, M_RCNT], small[5][:, :]).then_inc(dve_set, 1)
            dve.wait_ge(dve_set, next(set_step))
            V.tensor_scalar(out=small[5][:, :], in0=Dg[:, :], scalar1=float(WIN), scalar2=2.0, op0=ALU.is_ge, op1=ALU.mult).then_inc(dve_set, 1)
            dve.wait_ge(dve_set, next(set_step))
            V.tensor_scalar(out=tab[:, :, M_BOUND], in0=small[5][:, :], scalar1=-1.0, scalar2=FMAX, op0=ALU.add, op1=ALU.mult).then_inc(dve_set, 1)
            dve.wait_ge(dve_set, next(set_step))
            V.tensor_scalar(out=small[5][:, :], in0=B[:, :], scalar1=float(NE - WIN), scalar2=None, op0=ALU.min).then_inc(dve_set, 1)
            dve.wait_ge(dve_set, next(set_step))
            V.scalar_tensor_tensor(out=small[6][:, :], in0=E[:, :], scalar=float(-WIN), in1=B[:, :], op0=ALU.add, op1=ALU.max).then_inc(dve_set, 1)
            dve.wait_ge(dve_set, next(set_step))
            V.tensor_copy(tabi[:, :, 0], small[5][:, :]).then_inc(dve_set, 1)
            dve.wait_ge(dve_set, next(set_step))
            V.tensor_scalar(out=tabi[:, :, 1], in0=small[6][:, :], scalar1=float(NE - WIN), scalar2=None, op0=ALU.min).then_inc(dve_set, 1)
            dve.wait_ge(dve_set, next(set_step))
            V.tensor_tensor(out=small[6][:, :], in0=E[:, :], in1=small[5][:, :], op=ALU.subtract).then_inc(dve_set, 1)
            dve.wait_ge(dve_set, next(set_step))
            V.tensor_tensor(out=small[5][:, :], in0=B[:, :], in1=small[5][:, :], op=ALU.subtract).then_inc(dve_set, 1)
            dve.wait_ge(dve_set, next(set_step))
            sl = iota16[:, None, :].broadcast_to([P, NTP, WIN])
            V.tensor_tensor(out=m16[0], in0=sl, in1=small[6][:, :, None].broadcast_to([P, NTP, WIN]), op=ALU.is_ge).then_inc(dve_set, 1)
            dve.wait_ge(dve_set, next(set_step))
            V.tensor_tensor(out=m16[1], in0=sl, in1=small[5][:, :, None].broadcast_to([P, NTP, WIN]), op=ALU.is_lt).then_inc(dve_set, 1)
            dve.wait_ge(dve_set, next(set_step))
            V.tensor_tensor(out=m16[0], in0=m16[0], in1=m16[1], op=ALU.add).then_inc(dve_set, 1)
            dve.wait_ge(dve_set, next(set_step))
            V.tensor_scalar(out=m16[0], in0=m16[0], scalar1=-2.0, scalar2=1.0, op0=ALU.mult, op1=ALU.add).then_inc(dve_set, 1)
            dve.wait_ge(dve_set, next(set_step))
            V.tensor_scalar(out=tab[:, :, M_MASK:M_MASK + WIN], in0=m16[0], scalar1=FMAX, scalar2=None, op0=ALU.mult).then_inc(dve_set, 1)
            dve.wait_ge(dve_set, next(set_step))
            V.tensor_scalar(out=small[8][:, 0:NT], in0=mv[:, 0:NT, 1], scalar1=EPS, scalar2=None, op0=ALU.add).then_inc(var_ready, 1)
            dve.wait_ge(std_ready, 1)
            r0, a, v = small[6][:, 0:NT], small[5][:, 0:NT], small[8][:, 0:NT]
            V.reciprocal(r0, small[7][:, 0:NT]).then_inc(dve_set, 1)
            dve.wait_ge(dve_set, next(set_step))
            V.tensor_tensor(out=a, in0=r0, in1=r0, op=ALU.mult).then_inc(dve_set, 1)
            dve.wait_ge(dve_set, next(set_step))
            V.tensor_tensor(out=a, in0=a, in1=v, op=ALU.mult).then_inc(dve_set, 1)
            dve.wait_ge(dve_set, next(set_step))
            V.tensor_scalar(out=a, in0=a, scalar1=-0.5, scalar2=1.5, op0=ALU.mult, op1=ALU.add).then_inc(dve_set, 1)
            dve.wait_ge(dve_set, next(set_step))
            V.memset(tab[:, NT:NTP, M_RSTD:M_OFF + 1], 0.0).then_inc(dve_set, 1)
            dve.wait_ge(dve_set, next(set_step))
            V.tensor_tensor(out=tab[:, 0:NT, M_RSTD], in0=r0, in1=a, op=ALU.mult).then_inc(dve_set, 1)
            dve.wait_ge(dve_set, next(set_step))
            V.scalar_tensor_tensor(out=tab[:, 0:NT, M_OFF], in0=mv[:, 0:NT, 0], scalar=-1.0, in1=tab[:, 0:NT, M_RSTD], op0=ALU.mult, op1=ALU.mult).then_inc(dve_set, 1)
            dve.wait_ge(dve_set, next(set_step))
            dve.wait_ge(pe_set, 7)
            V.tensor_tensor(out=b1e[:, :], in0=tpr[:, 0:HC], in1=b1c[:, :], op=ALU.add).then_inc(dve_set, 1)
            dve.wait_ge(dve_set, next(set_step))
            dve.wait_ge(act_set, KC // 2 + 3)
            for c in range(0, KC, 2):
                V.tensor_tensor(out=w1l[:, c:c + 2, :], in0=rawf[c // 2][:, 0:2 * H].rearrange("p (c h) -> p c h", h=H), in1=w1h[:, c:c + 2, :], op=ALU.subtract)
            V.tensor_tensor(out=w1r[KR:2 * KR, :], in0=natf[0][KR:2 * KR, 0:H], in1=w1r[KR:2 * KR, :], op=ALU.subtract)
            for c in range(2):
                last = V.tensor_tensor(out=w2l[:, c * 4:(c + 1) * 4, :], in0=hfw[c], in1=w2h[:, c * 4:(c + 1) * 4, :], op=ALU.subtract)
            last.then_inc(setup_free, 1)
            dve.wait_ge(setup_free, 1)
            dve.wait_ge(flag_ready, 1)
            general = dve.value_load(flag[0:1, 0:1], min_val=0, max_val=1)
            with dve.If(general > 0):
                V.memset(sumT[0:F + 1, :], 0.0).then_inc(g_upd, 1)
                V.memset(maxT[0:F, :], -FMAX).then_inc(g_upd, 1)
                V.memset(eT[F:F + 1, :], 1.0).then_inc(g_upd, 1)
                with dve.Fori(0, NROW) as r:
                    dve.wait_ge(g_in, r * 32 + 32)
                    V.sem_inc(dve_turn, 1)
                    with dve.Fori(0, ROW) as j:
                        n = dve.value_load(gdst[0:1, bass.ds(j, 1)], min_val=0, max_val=N - 1)
                        V.drain()
                        V.tensor_tensor(out=sumT[0:F + 1, bass.ds(n, 1)], in0=sumT[0:F + 1, bass.ds(n, 1)], in1=eT[0:F + 1, bass.ds(j, 1)], op=ALU.add)
                        V.tensor_tensor(out=maxT[0:F, bass.ds(n, 1)], in0=maxT[0:F, bass.ds(n, 1)], in1=eT[0:F, bass.ds(j, 1)], op=ALU.max)
                    V.drain()
                    V.sem_inc(g_used, 1)
                V.sem_inc(g_done, 1)
                dve.wait_ge(gc_in, 32)
                V.tensor_scalar(out=small[5][:, :], in0=tab[:, :, M_ANY], scalar1=1.0, scalar2=None, op0=ALU.max).then_inc(g_upd, 1)
                dve.wait_ge(g_upd, 4)
                V.reciprocal(tab[:, :, M_RCNT], small[5][:, :]).then_inc(g_upd, 1)
                V.tensor_scalar(out=tab[:, :, M_ANY], in0=tab[:, :, M_ANY], scalar1=1.0, scalar2=None, op0=ALU.min).then_inc(g_upd, 1)
                dve.wait_ge(g_upd, 6)
            V.sem_inc(setup_free, 1)

            def lo(C):
                cols = columns(C)
                dve.wait_ge(hi_done, nth((C + 1) * 2))
                dve.wait_ge(l2_done, nth(C - 3))
                V.tensor_tensor(out=hl[C % 4][:, 0:cols], in0=hf[C % 2][:, 0:cols], in1=hh[C % 4][:, 0:cols], op=ALU.subtract).then_inc(lo_done, 1)

            def body(T):
                A = T + 2
                if is_tile(A):
                    dve.wait_ge(ndst_in[A % 4], nth((A // 4) * 16 + 16))
                    dve.wait_ge(stg_done, nth(A * 2 + 2))
                    dve.wait_ge(oh_done, nth(A))
                    V.tensor_scalar(out=dloc[:, :], in0=ndst[A % 4][:, :], scalar1=stg[A % 4][:, M_BASE:M_BASE + 1], scalar2=None, op0=ALU.subtract).then_inc(dloc_done, 1)
                    dve.wait_ge(dloc_done, nth(A + 1))
                    dve.wait_ge(sums_done, nth(A - 1))
                    V.tensor_tensor(out=onehot[A % 2][:, :, :], in0=iota[:, None, :].broadcast_to([P, NJ, P]),
                                    in1=dloc[:, :, None].broadcast_to([P, NJ, P]), op=ALU.is_equal).then_inc(oh_done, 1)
                M = T + 1
                e = ell[M % 2]
                s = stg[M % 4]
                if is_tile(M):
                    dve.wait_ge(ell_in[M % 2], nth((M // 2) * 32 + 32))
                    dve.wait_ge(stg_done, nth(M * 2 + 2))
                    V.tensor_tensor(out=e[:, 0:WIN, :], in0=e[:, 0:WIN, :], in1=s[:, M_MASK:M_MASK + WIN, None].broadcast_to([P, WIN, F]), op=ALU.min).then_inc(masked, 1)
                C = (T - 4) * 2
                if is_chunk(C):
                    lo(C)
                if is_tile(T):
                    b, k = (T // 4) % 2, T % 4
                    ks = slice(k * P, (k + 1) * P)
                    dve.wait_ge(hiT_done, nth(T * 2 + 2))
                    V.tensor_tensor(out=inl[b][:, :, ks], in0=tps[:, :].rearrange("p (c n) -> p c n", n=P), in1=inh[b][:, :, ks], op=ALU.subtract)
                    V.tensor_tensor(out=inr[b][2 * KR:3 * KR, ks], in0=tpr[2 * KR:3 * KR, 0:P], in1=inr[b][2 * KR:3 * KR, ks], op=ALU.subtract).then_inc(loT_done, 1)
                if is_tile(M):
                    dve.wait_ge(masked, nth(M + 1))
                    dve.wait_ge(max2, nth(M))
                    V.tensor_reduce(out=mx[:, 0, :], in_=e[:, 0:WIN, :].rearrange("p j f -> p f j"), axis=AX.X, op=ALU.max).then_inc(maxes, 1)
                    V.tensor_reduce(out=mx[:, 1, :], in_=e[:, WIN:2 * WIN, :].rearrange("p j f -> p f j"), axis=AX.X, op=ALU.max).then_inc(maxes, 1)
                    dve.wait_ge(maxes, nth(M * 2 + 2))
                    dve.wait_ge(out2_done, nth(M))
                    rounds = dve.value_load(rcum[0:1, 0, bass.ds(M.value, 1)], min_val=0, max_val=XR)
                    with dve.If(rounds > 0):
                        before = dve.value_load(rcum[0:1, 1, bass.ds(M.value, 1)], min_val=0, max_val=XR * NTP)
                        with dve.Fori(0, rounds) as q:
                            dve.wait_ge(x_in_w, (before + q) * 16 + 16)
                            dve.wait_ge(x_used, before + q + 1)
                            V.tensor_reduce(out=mxx[:, :], in_=xw.rearrange("p (j f) -> p f j", f=F), axis=AX.X, op=ALU.max).then_inc(x_red, 1)
                            dve.wait_ge(x_red, before + q + 1)
                            V.tensor_tensor(out=mx[:, 1, :], in0=mx[:, 1, :], in1=mxx[:, :], op=ALU.max).then_inc(x_used, 1)
                            dve.wait_ge(x_used, before + q + 2)
                            V.sem_inc(dve_turn, 1)
                    V.scalar_tensor_tensor(out=mx2[:, :], in0=mx[:, 1, :], scalar=s[:, M_BOUND:M_BOUND + 1], in1=mx[:, 0, :], op0=ALU.min, op1=ALU.max).then_inc(max2, 1)
                    dve.wait_ge(max2, nth(M + 1))
                    dve.wait_ge(trans_done, nth(M - 1))
                    V.tensor_scalar(out=cat[M % 2][:, D + F:D + 2 * F], in0=mx2[:, :], scalar1=s[:, M_ANY:M_ANY + 1], scalar2=None, op0=ALU.mult).then_inc(gmix, 1)
                    dve.wait_ge(gmix, nth(M + 1))
                    V.sem_inc(dve_turn, 1)
                    with dve.If(general > 0):
                        dve.wait_ge(outs_done, nth(M + 1))
                        dve.wait_ge(gt_in, nth(M * 32 + 32))
                        c = cat[M % 2]
                        rc = s[:, M_RCNT:M_RCNT + 1]
                        V.tensor_copy(c[:, D:D + F], gst[:, 0, :])
                        V.tensor_scalar(out=c[:, D + F:D + 2 * F], in0=gst[:, 1, :], scalar1=s[:, M_ANY:M_ANY + 1], scalar2=None, op0=ALU.mult)
                        V.tensor_scalar(out=c[:, D + 2 * F:KC * P], in0=gst[:, 0, 0:F - KR], scalar1=rc, scalar2=None, op0=ALU.mult)
                        V.tensor_scalar(out=c[:, KC * P:CAT].rearrange("p (r k) -> p r k", k=KR), in0=gst[:, 0, None, F - KR:F].broadcast_to([P, 3, KR]),
                                        scalar1=rc, scalar2=None, op0=ALU.mult).then_inc(gt_used, 1)
                        dve.wait_ge(gt_used, nth(M + 1))
                        V.sem_inc(dve_turn, 1)
                    V.sem_inc(out2_done, 1)
                if is_chunk(C + 1):
                    lo(C + 1)
            steps(dve, body)


_INS = ["x", "dst", "edge_attr_96", "L0_gnn_u", "L0_gnn_W1", "L0_gnn_b1", "L0_gnn_W2", "L0_gnn_b2"]


def kernel(**inputs):
    import numpy as _np
    import concourse.bacc as _bacc
    from concourse import mybir as _mybir
    from concourse.bass_utils import run_bass_kernel_spmd as _run

    nc = _bacc.Bacc("TRN2", target_bir_lowering=False, num_devices=1)
    arrays, args = {}, []
    for name in _INS:
        a = _np.ascontiguousarray(inputs[name])
        arrays[f"in_{name}"] = a
        args.append(nc.dram_tensor(f"in_{name}", a.shape, _mybir.dt.from_np(a.dtype), kind="ExternalInput").ap())
    shape = inputs["x"].shape
    args.append(nc.dram_tensor("out_y", shape, _mybir.dt.float32, kind="ExternalOutput").ap())
    gnn_block(nc, *args)
    r = _run(nc, [arrays], core_ids=[0])
    return r.results[0]["out_y"]
```

```python
import itertools

import concourse.bass as bass
from concourse import mybir

P = 128


class Step:

    def __init__(self, const, coef=0, reg=None):
        self.const, self.coef, self.reg = const, coef, reg

    def __add__(self, n):
        return Step(self.const + n, self.coef, self.reg)

    def __sub__(self, n):
        return self + (-n)

    def __mul__(self, n):
        return Step(self.const * n, self.coef * n, self.reg)

    def __floordiv__(self, n):
        assert self.coef % n == 0
        return Step(self.const // n, self.coef // n, self.reg)

    def __mod__(self, n):
        assert self.coef % n == 0
        return self.const % n

    @property
    def value(self):
        return self.const if not self.coef else self.reg * self.coef + self.const


def nth(count):
    if isinstance(count, Step):
        if count.coef:
            assert count.const > 0
            return count.value
        count = count.const
    return max(count, 0)


def gnn_block(nc, x, dst, edge, u, W1, b1, W2, b2, out):
    f32, f32r, i32 = mybir.dt.float32, mybir.dt.float32r, mybir.dt.int32
    ALU, ACT, AX = mybir.AluOpType, mybir.ActivationFunctionType, mybir.AxisListType

    N, D = x.shape
    NE, F = edge.shape
    G = u.shape[1]
    H = W1.shape[1]
    NT = -(-N // P)
    NTP = NT + 1
    BT = 4
    NB = -(-NT // BT)
    HC = H // P
    K = D + 3 * F
    assert K + G == W1.shape[0]
    KC = K // P
    KR = K - KC * P
    CAT = KC * P + 3 * KR
    NJ = 19
    CAPE = NJ * P
    WIN = 16
    XW = 8
    XR = 8
    ROW = 425
    NROW = NE // ROW
    assert NROW * ROW == NE
    LAST = N - (NT - 1) * P
    FMAX = 3.3895e38
    EPS = 1e-5

    sb = {}

    def sbuf(name, shape, dt=f32):
        sb[name] = nc.alloc_sbuf_tensor(name, shape, dt)
        return sb[name]

    w1h, w1l = sbuf("w1h", [P, KC, H], f32r), sbuf("w1l", [P, KC, H], f32r)
    w1r = sbuf("w1r", [3 * KR, H], f32r)
    w2h, w2l = sbuf("w2h", [P, HC, D], f32r), sbuf("w2l", [P, HC, D], f32r)
    b1e, b2b = sbuf("b1e", [P, HC]), sbuf("b2b", [P, D])
    inh = [sbuf(f"inh{i}", [P, KC, BT * P], f32r) for i in range(2)]
    inl = [sbuf(f"inl{i}", [P, KC, BT * P], f32r) for i in range(2)]
    inr = [sbuf(f"inr{i}", [3 * KR, BT * P], f32r) for i in range(2)]
    hf = [sbuf(f"hf{i}", [P, BT * P]) for i in range(2)]
    hh = [sbuf(f"hh{i}", [P, BT * P], f32r) for i in range(4)]
    hl = [sbuf(f"hl{i}", [P, BT * P], f32r) for i in range(4)]
    natn, ohn, elln = NJ * F, NJ * P, 2 * WIN * F
    work = sbuf("work", [P, 2 * (natn + ohn + elln)])
    natf = [work[:, i * natn:(i + 1) * natn] for i in range(2)]
    nat = [t.rearrange("p (j f) -> p j f", f=F) for t in natf]
    ohf = [work[:, 2 * natn + i * ohn:2 * natn + (i + 1) * ohn] for i in range(2)]
    onehot = [t.rearrange("p (j n) -> p j n", n=P) for t in ohf]
    ellf = [work[:, 2 * (natn + ohn) + i * elln:2 * (natn + ohn) + (i + 1) * elln] for i in range(2)]
    ell = [t.rearrange("p (j f) -> p j f", f=F) for t in ellf]
    ndst = [sbuf(f"ndst{i}", [P, NJ], i32) for i in range(4)]
    dloc = sbuf("dloc", [P, NJ])
    mxx = sbuf("mxx", [P, F])
    wmask = sbuf("wmask", [P, 2, WIN])
    cat = [sbuf(f"cat{i}", [P, CAT]) for i in range(2)]
    xin = [sbuf(f"xin{i}", [P, D]) for i in range(2)]
    xball = sbuf("xb", [P, 8 * D])
    xb = [xball[:, i * D:(i + 1) * D] for i in range(8)]
    yc = sbuf("yc", [P, 4, D])
    yo = sbuf("yo", [P, 4, D])
    M_B, M_XB, M_ANY, M_RCNT, M_BASE, M_RSTD, M_OFF, M_S, M_E8, M_LO, M_HI, NM = 0, 4, 5, 6, 7, 8, 9, 10, 11, 12, 14, 16
    tab = sbuf("tab", [P, NTP, NM])
    tabi = sbuf("tabi", [P, NTP, 2], i32)
    stg = [sbuf(f"stg{i}", [P, NM]) for i in range(4)]
    stgi = [sbuf(f"stgi{i}", [P, 2], i32) for i in range(4)]
    ident = sbuf("ident", [P, P])
    iota = sbuf("iota", [P, P])
    e0row = sbuf("e0row", [1, NTP], i32)
    rawf = ohf
    scratch = sbuf("scratch", [P, 20 * NTP])
    cols = [scratch[:, i * NTP:(i + 1) * NTP] for i in range(20)]
    nid, cnt1, cnt2, rowi = cols[0], cols[1], cols[2], cols[3].bitcast(i32)
    rows = [natf[1][:, i * ROW:(i + 1) * ROW].bitcast(i32) for i in range(4)]
    hfw = [yc[:, :, :], yo[:, :, :]]
    small = cols[4:13]
    Dg = small[4]
    stats = scratch[:, 13 * NTP:13 * NTP + 6 * NT].rearrange("p (t s) -> p t s", s=6)
    mv = sbuf("mv", [P, NTP, 2])
    pid = sbuf("pid", [P, 1])
    shift = sbuf("shift", [NTP, NTP])
    ones = sbuf("ones", [1, P])
    fi = yo[0:1, 0, 0:NROW].bitcast(i32)
    ff = yo[0:1, 1, 0:NROW]
    trisb = sbuf("tri", [NTP, NTP])
    rcum = sbuf("rcum", [1, 4, NTP], i32)
    flag = sbuf("flag", [1, 1], i32)
    onesc = sbuf("onesc", [P, 1])
    bad = sbuf("bad", [P, 2])
    dm = sbuf("dm", [NTP, 8])
    xi, xif = sbuf("xi", [P, 1], i32), sbuf("xif", [P, 2])
    xw = scratch[:, 0:XW * F]
    gst = sbuf("gst", [P, 2, F])
    sumT, maxT = work[:, 0:NT * P], work[:, NT * P:2 * NT * P]
    eT = work[:, 2 * NT * P:2 * NT * P + ROW]
    gdst = work[0:1, 2 * NT * P + ROW:2 * NT * P + 2 * ROW].bitcast(i32)
    fb = hf[1][:, 0:NROW]
    et, st = sbuf("et", [NTP, P]), sbuf("st", [NTP, P])
    iota16 = sbuf("iota16", [P, WIN])
    u0 = sbuf("u0", [G, 1])
    w1u = ellf[0][0:G, 7 * D:7 * D + H]
    b1c = sbuf("b1c", [P, HC])
    junka = [sbuf(f"junka{i}", [P, ROW]) for i in range(2)]
    nidh = sbuf("nidh", [P, NTP])
    junk = [ellf[1][:, 7 * D:7 * D + ROW], hf[0][:, 0:ROW]]

    def psum(name, shape):
        return nc.alloc_psum_tensor(name, shape, f32)

    l1ps = [psum(f"l1ps{i}", [P, BT * P]) for i in range(2)]
    yps = [psum(f"yps{i}", [P, 2 * D]) for i in range(2)]
    tps, tpr = psum("tps", [P, BT * P]), psum("tpr", [P, BT * P])
    sps = [psum(f"sps{i}", [P, 512]) for i in range(2)]

    S = nc.alloc_semaphore
    w_in, r_in, w2_in, c_in = S("w_in"), S("r_in"), S("w2_in"), S("c_in")
    consts, f_in, f_row, f_ps, f_sb = S("consts"), S("f_in"), S("f_row"), S("f_ps"), S("f_sb")
    cnt1_done, row_done, rowbuf_used = S("cnt1_done"), S("row_done"), S("rowbuf_used")
    cnt1_act, rowbuf_act, nid_half = S("cnt1_act"), S("rowbuf_act"), S("nid_half")
    rnd_in = S("rnd_in")
    rowbuf_in = [S(f"rows_or_stores{i}") for i in range(4)]
    dve_set, pe_set, act_set, pool_set = S("dve_set"), S("pe_set"), S("act_set"), S("pool_set")
    xs_in = [S(f"xs_in{i}") for i in range(2)]
    xs_used, e0_ready, setup_free = S("xs_used"), S("e0_ready"), S("setup_free")
    var_ready, std_ready = S("var_ready"), S("std_ready")
    ends_ready, et_ready, st_ready, dcol_ready = S("ends_ready"), S("et_ready"), S("st_ready"), S("dcol_ready")
    nat_in = [S(f"nat_in{i}") for i in range(2)]
    ndst_in = [S(f"ndst_in{i}") for i in range(4)]
    x_in = [S(f"x_in{i}") for i in range(2)]
    ell_in = [S(f"ell_in{i}") for i in range(2)]
    dloc_done, oh_done, sums_done, trans_done = S("dloc_done"), S("oh_done"), S("sums_done"), S("trans_done")
    l1_done, l2_done = S("l1_done"), S("l2_done")
    hi_done, lo_done, hiT_done, loT_done = S("hi_done"), S("lo_done"), S("hiT_done"), S("loT_done")
    h_done, outs_done, masked, levels, max2, out2_done = (S(n) for n in
        ("h_done", "outs_done", "masked", "levels", "max2", "out2_done"))
    stg_done, xb_part, xb_done, add_done, evac_done = (S(n) for n in
        ("stg_done", "xb_part", "xb_done", "add_done", "evac_done"))
    gmix, dve_turn = S("gmix"), S("dve_turn")
    pool_turn, sd_in, x_idx, x_in_w, x_red, x_used = (S(n) for n in ("pool_turn", "sd_in", "x_idx", "x_in_w", "x_red", "x_used"))
    flag_ready, g_in, g_used, g_upd, g_done, g_out, gc_in, gt_in, gt_used = (S(n) for n in
        ("flag_ready", "g_in", "g_used", "g_upd", "g_done", "g_out", "gc_in", "gt_in", "gt_used"))
    stored = rowbuf_in
    gathered = [16 * len(range(r, NTP, 4)) for r in range(4)]

    edge_rows = edge
    gsum = nc.dram_tensor("gsum", [NT * P, F], f32, kind="Internal").ap()
    gmax = nc.dram_tensor("gmax", [NT * P, F], f32, kind="Internal").ap()
    gcnt = nc.dram_tensor("gcnt", [1, NT * P], f32, kind="Internal").ap()
    dst_row = dst.rearrange("(r c) -> r c", c=ROW)

    SC = 2 * ROW
    SR = NE // SC
    assert SR * SC == NE and SR <= P and SC < 4 * D
    sd = xball[:, 0:SC + 1].bitcast(i32)
    sbad = xball[:, 4 * D:4 * D + SC]

    XG = 7
    XGF = NT // XG
    assert XGF * XG == NT
    xs = [ellf[i][:, 0:XG * D].rearrange("p (t d) -> p t d", d=D) for i in range(2)]

    def steps(eng, body):
        for t in range(-2, 8):
            body(Step(t))
        with eng.Fori(0, 5) as i:
            for t in range(8, 16):
                body(Step(t, 8, i))
        for t in range(48, 57):
            body(Step(t))

    def is_tile(T, n=NT):
        return bool(T.coef) or 0 <= T.const < n

    def is_chunk(C):
        return bool(C.coef) or 0 <= C.const < NC_ALL

    NC_ALL = HC * NB

    def columns(C):
        return P if (not C.coef and C.const // HC == NB - 1) else BT * P

    with nc.Block() as block:

        @block.sync
        def _(sp):
            sp.dma_start(fi, dst_row[:, 0:1].rearrange("r c -> c r"), allow_slow_non_contiguous=True).then_inc(f_in, 16)
            def load_x(g):
                sp.wait_ge(xs_used, nth((g - 1) * XG))
                full = XG if g < XGF - 1 else XG - 1
                sp.dma_start(xs[g % 2][:, 0:full, :],
                             x[g * XG * P:(g * XG + full) * P, :].rearrange("(t p) d -> p t d", p=P)).then_inc(xs_in[g % 2], 16)
                if full < XG:
                    sp.dma_start(xs[g % 2][0:LAST, full, :], x[(NT - 1) * P:N, :]).then_inc(xs_in[g % 2], 16)
            sp.dma_start(sd[0:SR, 0:SC], dst.rearrange("(r c) -> r c", c=SC)).then_inc(sd_in, 16)
            sp.wait_ge(consts, 9)
            sp.dma_start(sd[0:SR - 1, SC:SC + 1], dst.rearrange("(r c) -> r c", c=SC)[1:SR, 0:1], allow_slow_non_contiguous=True).then_inc(sd_in, 16)
            load_x(0)
            load_x(1)
            for c in range(0, KC, 2):
                sp.dma_start(rawf[c // 2][:, 0:2 * H].rearrange("p (c h) -> p c h", h=H),
                             W1[c * P:(c + 2) * P, :].rearrange("(c p) h -> p c h", p=P)).then_inc(w_in, 16)
            for r in range(3):
                sp.dma_start(natf[0][r * KR:(r + 1) * KR, 0:H], W1[KC * P:K, :]).then_inc(r_in, 16)
            sp.wait_ge(f_ps, 1)
            for c in range(2):
                sp.dma_start(hfw[c], W2[c * 4 * P:(c + 1) * 4 * P, :].rearrange("(c p) d -> p c d", p=P)).then_inc(w2_in, 16)
            sp.dma_start(w1u, W1[K:K + G, :]).then_inc(c_in, 16)
            sp.dma_start(u0[:, :], u[0:1, :].rearrange("a g -> g a"), allow_slow_non_contiguous=True).then_inc(c_in, 16)
            sp.dma_start(b1c[:, :], b1.rearrange("(c p) -> p c", p=P), allow_slow_non_contiguous=True).then_inc(c_in, 16)
            sp.dma_start(b2b[:, :], b2.rearrange("(a d) -> a d", a=1).broadcast_to([P, D])).then_inc(c_in, 16)
            for g in range(2, XGF):
                load_x(g)
            sp.wait_ge(e0_ready, 1)
            sp.wait_ge(setup_free, 1)
            sp.wait_ge(flag_ready, 1)
            general = sp.value_load(flag[0:1, 0:1], min_val=0, max_val=1)
            with sp.If(general > 0):
                with sp.Fori(0, NROW) as r:
                    sp.wait_ge(g_used, r + 1)
                    sp.dma_start(gdst, dst_row[bass.ds(r, 1), :]).then_inc(g_in, 16)
                    sp.dma_start(eT[0:F, :], edge[bass.ds(r * ROW, ROW), :].rearrange("e f -> f e"), allow_slow_non_contiguous=True).then_inc(g_in, 16)
                sp.wait_ge(g_done, 1)
                sp.dma_start(gsum.rearrange("n f -> f n"), sumT[0:F, :], allow_slow_non_contiguous=True).then_inc(g_out, 16)
                sp.dma_start(gmax.rearrange("n f -> f n"), maxT[0:F, :], allow_slow_non_contiguous=True).then_inc(g_out, 16)
                sp.dma_start(gcnt, sumT[F:F + 1, :]).then_inc(g_out, 16)
                sp.wait_ge(g_out, 48)
                sp.dma_start(tab[:, 0:NT - 1, M_ANY], gcnt[0:1, 0:(NT - 1) * P].rearrange("a (t p) -> (a p) t", p=P), allow_slow_non_contiguous=True).then_inc(gc_in, 16)
                sp.dma_start(tab[0:LAST, NT - 1:NT, M_ANY], gcnt[0:1, (NT - 1) * P:N].rearrange("a (t p) -> (a p) t", t=1), allow_slow_non_contiguous=True).then_inc(gc_in, 16)
            sp.wait_ge(setup_free, 2)

            def body(T):
                D2 = T + 2
                if is_tile(D2, NTP):
                    sp.wait_ge(dloc_done, nth(D2 - 3))
                    first = sp.value_load(e0row[0:1, bass.ds(D2.value, 1)], min_val=0, max_val=NE - CAPE)
                    sp.dma_start(ndst[D2 % 4][:, :], dst[bass.ds(first, CAPE)].rearrange("(p j) -> p j", j=NJ)).then_inc(ndst_in[D2 % 4], 16)
                G = T + 1
                if is_tile(G):
                    with sp.If(general > 0):
                        sp.wait_ge(gt_used, nth(G))
                        n = P if (G.coef or G.const < NT - 1) else LAST
                        at = bass.ds(G.value * P, P) if G.coef else slice(G.const * P, G.const * P + n)
                        sp.dma_start(gst[0:n, 0, :], gsum[at, :]).then_inc(gt_in, 16)
                        sp.dma_start(gst[0:n, 1, :], gmax[at, :]).then_inc(gt_in, 16)
                if is_tile(T):
                    first = sp.value_load(e0row[0:1, bass.ds(T.value, 1)], min_val=0, max_val=NE - CAPE)
                    sp.wait_ge(sums_done, nth(T - 1))
                    sp.dma_start(nat[T % 2][:, :, :], edge_rows[bass.ds(first, CAPE), :].rearrange("(p j) f -> p j f", j=NJ)).then_inc(nat_in[T % 2], 16)
                    sp.wait_ge(xb_done, nth(T - 1))
                    sp.wait_ge(h_done, nth(T - 1))
                    if T.coef or T.const < NT - 1:
                        sp.dma_start(xin[T % 2][:, :], x[bass.ds(T.value * P, P), :] if T.coef else x[T.const * P:(T.const + 1) * P, :]).then_inc(x_in[T % 2], 16)
                    else:
                        sp.dma_start(xin[T % 2][0:LAST, :], x[T.const * P:N, :]).then_inc(x_in[T % 2], 16)
            steps(sp, body)

        @block.gpsimd
        def _(pool):
            kw = dict(allow_small_or_imprecise_dtypes=True)
            pool.sem_inc(add_done, 1)
            pool.iota(iota[:, :], pattern=[[1, P]], base=0, channel_multiplier=0, **kw).then_inc(consts, 1)
            pool.iota(pid[:, :], pattern=[[1, 1]], base=0, channel_multiplier=1, **kw).then_inc(consts, 1)
            pool.iota(nid[:, :], pattern=[[P, NTP]], base=0, channel_multiplier=1, **kw).then_inc(consts, 1)
            pool.iota(iota16[:, :], pattern=[[1, WIN]], base=0, channel_multiplier=0, **kw).then_inc(consts, 1)
            pool.iota(tab[:, :, M_BASE], pattern=[[P, NTP]], base=0, channel_multiplier=0, **kw).then_inc(consts, 1)
            pool.memset(ones[:, :], 1.0).then_inc(consts, 1)
            pool.memset(sd[:, SC:SC + 1], N).then_inc(consts, 1)
            pool.memset(onesc[:, :], 1.0).then_inc(consts, 1)
            pool.memset(bad[:, :], 0.0).then_inc(consts, 1)
            for t in range(NTP):
                pool.wait_ge(row_done, nth(t // 10 + 1 if t % 10 == 0 else 0))
                pool.wait_ge(rowbuf_act if t % 2 else rowbuf_used, nth((t - 4) // 2 + 1))
                pool.indirect_dma_start(out=rows[t % 4], out_offset=None, in_=dst_row,
                                        in_offset=bass.IndirectOffsetOnAxis(ap=rowi[:, t:t + 1], axis=0)).then_inc(rowbuf_in[t % 4], 16)
            for r in range(4):
                pool.wait_ge(rowbuf_in[r], gathered[r])
            pool.wait_ge(act_set, KC // 2 + 3)
            for c in range(0, KC, 2):
                pool.tensor_tensor(out=w1l[:, c:c + 2, :], in0=rawf[c // 2][:, 0:2 * H].rearrange("p (c h) -> p c h", h=H), in1=w1h[:, c:c + 2, :], op=ALU.subtract).then_inc(pool_set, 1)
            pool.wait_ge(pool_set, KC // 2)
            pool.tensor_tensor(out=w1r[KR:2 * KR, :], in0=natf[0][KR:2 * KR, 0:H], in1=w1r[KR:2 * KR, :], op=ALU.subtract).then_inc(pool_set, 1)
            pool.wait_ge(pool_set, KC // 2 + 1)
            for c in range(2):
                pool.tensor_tensor(out=w2l[:, c * 4:(c + 1) * 4, :], in0=hfw[c], in1=w2h[:, c * 4:(c + 1) * 4, :], op=ALU.subtract).then_inc(pool_set, 1)
            pool.wait_ge(setup_free, 2)

            def body(T):
                A = T + 2
                if is_tile(A, NTP):
                    pool.wait_ge(outs_done, nth(A - 3))
                    pool.wait_ge(out2_done, nth(A - 3))
                    pool.wait_ge(gmix, nth(A - 1))
                    pool.sem_inc(pool_turn, 1)
                    at = A.value
                    pool.tensor_copy(stg[A % 4][:, :], tab[:, bass.ds(at, 1), :]).then_inc(stg_done, 1)
                    pool.tensor_copy(stgi[A % 4][:, :], tabi[:, bass.ds(at, 1), :]).then_inc(stg_done, 1)
                    pool.wait_ge(stg_done, nth(A * 2 + 2))
                    pool.sem_inc(pool_turn, 1)
                    for w in range(2):
                        pool.indirect_dma_start(out=ellf[A % 2][:, w * WIN * F:(w + 1) * WIN * F], out_offset=None, in_=edge,
                                                in_offset=bass.IndirectOffsetOnAxis(ap=stgi[A % 4][:, w:w + 1], axis=0)).then_inc(ell_in[A % 2], 16)
                    rounds = pool.value_load(rcum[0:1, 0, bass.ds(at, 1)], min_val=0, max_val=XR)
                    with pool.If(rounds > 0):
                        before = pool.value_load(rcum[0:1, 1, bass.ds(at, 1)], min_val=0, max_val=XR * NTP)
                        g = stg[A % 4]
                        pool.tensor_scalar(out=xif[:, 0:1], in0=g[:, M_S:M_S + 1], scalar1=float(WIN - XW), scalar2=None, op0=ALU.add).then_inc(pool_turn, 1)
                        with pool.Fori(0, rounds) as q:
                            pool.wait_ge(x_used, before + q + 1)
                            pool.sem_inc(pool_turn, 1)
                            pool.drain()
                            pool.tensor_scalar(out=xif[:, 0:1], in0=xif[:, 0:1], scalar1=float(XW), scalar2=None, op0=ALU.add).then_inc(x_idx, 1)
                            pool.wait_ge(x_idx, (before + q) * 3 + 1)
                            pool.sem_inc(pool_turn, 1)
                            pool.tensor_scalar(out=xif[:, 1:2], in0=xif[:, 0:1], scalar1=g[:, M_E8:M_E8 + 1], scalar2=g[:, M_S:M_S + 1], op0=ALU.min, op1=ALU.max).then_inc(x_idx, 1)
                            pool.wait_ge(x_idx, (before + q) * 3 + 2)
                            pool.sem_inc(pool_turn, 1)
                            pool.tensor_scalar(out=xi[:, :], in0=xif[:, 1:2], scalar1=float(NE - XW), scalar2=None, op0=ALU.min).then_inc(x_idx, 1)
                            pool.wait_ge(x_idx, (before + q) * 3 + 3)
                            pool.sem_inc(pool_turn, 1)
                            pool.indirect_dma_start(out=xw, out_offset=None, in_=edge,
                                                    in_offset=bass.IndirectOffsetOnAxis(ap=xi[:, 0:1], axis=0)).then_inc(x_in_w, 16)
                U = T - 8
                if is_tile(U):
                    rows_ = P if (U.coef or U.const < NT - 1) else LAST
                    pool.wait_ge(evac_done, nth(U + 1))
                    pool.wait_ge(stored[U % 4], nth((U // 4) * 16 + gathered[U % 4]))
                    pool.tensor_tensor(out=yo[:, U % 4, :], in0=yc[:, U % 4, :], in1=xb[U % 8][:, :], op=ALU.add).then_inc(add_done, 1)
                    pool.wait_ge(add_done, nth(U + 2))
                    pool.sem_inc(pool_turn, 1)
                    where = out[bass.ds(U.value * P, P), :] if U.coef else out[U.const * P:U.const * P + rows_, :]
                    pool.dma_start(where, yo[0:rows_, U % 4, :]).then_inc(stored[U % 4], 16)
                if is_tile(T):
                    pool.wait_ge(h_done, nth(T + 1))
                    pool.wait_ge(xb_part, nth(T))
                    pool.wait_ge(add_done, nth(T - 6))
                    pool.tensor_tensor(out=xb[T % 8][:, :], in0=xin[T % 2][:, :], in1=cat[T % 2][:, 0:D], op=ALU.add).then_inc(xb_part, 1)
                    pool.wait_ge(xb_part, nth(T + 1))
                    pool.tensor_tensor(out=xb[T % 8][:, :], in0=xb[T % 8][:, :], in1=b2b[:, :], op=ALU.add).then_inc(xb_done, 1)
            pool.wait_ge(c_in, 64)
            steps(pool, body)
            for r in range(4):
                pool.wait_ge(stored[r], nth(16 * len(range(r, NT, 4)) + gathered[r]))
            for r in range(2):
                pool.wait_ge(ell_in[r], nth(32 * len(range(r, NTP, 2))))

        @block.scalar
        def _(act):
            act.wait_ge(nid_half, 1)
            act.wait_ge(f_ps, 1)
            for t in range(1, NTP, 2):
                act.wait_ge(cnt1_act, nth(t // 2 - 1))
                act.activation(junka[t // 2 % 2][:, 0:NROW], tps[:, 0:NROW], ACT.Sign, bias=nidh[:, t:t + 1], scale=-1.0,
                               accum_out=cnt1[:, t:t + 1]).then_inc(cnt1_act, 1)
            for c in range(0, KC, 2):
                act.wait_ge(w_in, 8 * KC)
                act.activation(w1h[:, c:c + 2, :], rawf[c // 2][:, 0:2 * H].rearrange("p (c h) -> p c h", h=H), ACT.Copy).then_inc(act_set, 1)
            act.wait_ge(r_in, 48)
            act.activation(w1r[:, :], natf[0][0:3 * KR, 0:H], ACT.Copy).then_inc(act_set, 1)
            act.wait_ge(w2_in, 32)
            for c in range(2):
                act.activation(w2h[:, c * 4:(c + 1) * 4, :], hfw[c], ACT.Copy).then_inc(act_set, 1)
            for t in range(1, NTP, 2):
                act.wait_ge(rowbuf_in[t % 4], 16 * (t // 4 + 1))
                act.wait_ge(rowbuf_act, nth(t // 2 - 1))
                if t == 1:
                    act.wait_ge(cnt1_act, NTP // 2)
                act.activation(junka[t // 2 % 2][:, :], rows[t % 4], ACT.Sign, bias=nidh[:, t:t + 1], scale=-1.0,
                               accum_out=cnt2[:, t:t + 1]).then_inc(rowbuf_act, 1)
            act.wait_ge(var_ready, 1)
            act.activation(small[7][:, 0:NT], small[8][:, 0:NT], ACT.Sqrt).then_inc(std_ready, 1)
            act.wait_ge(setup_free, 2)

            def relu(C):
                cols = columns(C)
                m = C % HC
                act.wait_ge(l1_done, nth(C + 1))
                act.wait_ge(lo_done, nth(C - 1))
                act.activation(hf[C % 2][:, 0:cols], l1ps[C % 2][:, 0:cols], ACT.Relu, bias=b1e[:, m:m + 1]).then_inc(hi_done, 1)
                act.wait_ge(l2_done, nth(C - 3))
                act.activation(hh[C % 4][:, 0:cols], l1ps[C % 2][:, 0:cols], ACT.Relu, bias=b1e[:, m:m + 1]).then_inc(hi_done, 1)

            def body(T):
                C = (T - 4) * 2
                if is_chunk(C):
                    relu(C)
                if is_tile(T):
                    b, k = (T // 4) % 2, T % 4
                    act.wait_ge(trans_done, nth(T + 1))
                    act.activation(inh[b][:, :, k * P:(k + 1) * P], tps[:, :].rearrange("p (c n) -> p c n", n=P), ACT.Copy).then_inc(hiT_done, 1)
                    act.activation(inr[b][:, k * P:(k + 1) * P], tpr[0:3 * KR, 0:P], ACT.Copy).then_inc(hiT_done, 1)
                A = T + 1
                if is_tile(A):
                    act.wait_ge(x_in[A % 2], nth((A // 2) * 16 + 16))
                    act.wait_ge(stg_done, nth(A * 2 + 2))
                    act.wait_ge(trans_done, nth(A - 1))
                    act.wait_ge(xb_done, nth(A - 1))
                    act.activation(cat[A % 2][:, 0:D], xin[A % 2][:, :], ACT.Relu, bias=stg[A % 4][:, M_OFF:M_OFF + 1],
                                   scale=stg[A % 4][:, M_RSTD:M_RSTD + 1]).then_inc(h_done, 1)
                if T % 4 == 0 and is_chunk(C - HC):
                    first = T - 8
                    act.wait_ge(l2_done, nth((T // 4 - 1) * HC))
                    act.wait_ge(add_done, nth(first + 1))
                    for j in range(BT if (T.coef or T.const < 56) else 1):
                        act.activation(yc[:, j, :], yps[j // 2][:, (j % 2) * D:(j % 2 + 1) * D], ACT.Copy).then_inc(evac_done, 1)
                if is_chunk(C + 1):
                    relu(C + 1)
                if is_tile(A):
                    q = sps[A % 2]
                    c, s = cat[A % 2], stg[A % 4]
                    act.wait_ge(sums_done, nth(A + 1))
                    act.activation(c[:, D:D + F], q[:, 0:F], ACT.Copy)
                    act.activation(c[:, D + 2 * F:KC * P], q[:, 0:F - KR], ACT.Copy, scale=s[:, M_RCNT:M_RCNT + 1])
                    act.activation(c[:, KC * P:CAT].rearrange("p (r k) -> p r k", k=KR), q[:, None, F - KR:F].broadcast_to([P, 3, KR]),
                                   ACT.Copy, scale=s[:, M_RCNT:M_RCNT + 1]).then_inc(outs_done, 1)
            steps(act, body)

        @block.tensor
        def _(pe):
            pe.wait_ge(f_row, 1)
            pe.wait_ge(consts, 9)
            pe.matmul(tps[:, 0:NROW], ones[0:1, :], ff, start=True, stop=True).then_inc(f_ps, 1)
            pe.wait_ge(ends_ready, 1)
            pe.transpose(sps[0][0:NTP, 0:P], small[0][:, 0:NTP], ident[:, :]).then_inc(pe_set, 1)
            pe.wait_ge(et_ready, 1)
            pe.matmul(sps[1][0:NTP, 0:1], shift[:, :], et[:, P - 1:P], start=True, stop=True).then_inc(pe_set, 1)
            pe.matmul(l1ps[0][0:1, 0:NTP], et[:, P - 1:P], shift[:, :], start=True, stop=True).then_inc(pe_set, 1)
            pe.wait_ge(st_ready, 1)
            pe.transpose(l1ps[1][:, 0:NTP], st[:, :], ident[0:NTP, 0:NTP]).then_inc(pe_set, 1)
            pe.wait_ge(dcol_ready, 1)
            pe.transpose(sps[0][0:NTP, 0:P], Dg[:, :], ident[:, :]).then_inc(pe_set, 1)
            pe.wait_ge(dcol_ready, 2)
            pe.matmul(l1ps[0][0:1, 0:NTP], dm[:, 1:2], ident[0:NTP, 0:NTP], start=True, stop=True)
            pe.matmul(l1ps[0][0:1, 64:64 + NTP], dm[:, 4:5], ident[0:NTP, 0:NTP], start=True, stop=True)
            pe.matmul(l1ps[0][0:1, 128:128 + NTP], dm[:, 5:6], ident[0:NTP, 0:NTP], start=True, stop=True)
            pe.matmul(sps[1][0:1, 0:NTP], dm[:, 1:2], trisb[:, :], start=True, stop=True)
            pe.matmul(sps[0][0:1, 0:2], onesc[:, :], bad[:, :], start=True, stop=True).then_inc(pe_set, 1)
            pe.wait_ge(c_in, 64)
            for m in range(HC):
                last = pe.matmul(tpr[:, m:m + 1], w1u[:, m * P:(m + 1) * P], u0[:, :], start=True, stop=True)
            last.then_inc(pe_set, 1)
            pe.wait_ge(setup_free, 2)

            def layer1(C):
                b, m, cols = (C // HC) % 2, C % HC, columns(C)
                pe.wait_ge(hi_done, nth((C - 1) * 2))
                first = True
                ms = slice(m * P, (m + 1) * P)
                for c in range(KC):
                    for wt, it in ((w1h, inh), (w1l, inh), (w1h, inl)):
                        pe.matmul(l1ps[C % 2][:, 0:cols], wt[:, c, ms], it[b][:, c, 0:cols], start=first, stop=False)
                        first = False
                pe.matmul(l1ps[C % 2][:, 0:cols], w1r[:, ms], inr[b][:, 0:cols], start=False, stop=True).then_inc(l1_done, 1)

            def layer2(C):
                m, cols = C % HC, columns(C)
                pe.wait_ge(lo_done, nth(C + 1))
                if m == 0:
                    pe.wait_ge(evac_done, nth((C // HC) * 4))
                for j in range(cols // P):
                    for ht, wt in ((hh, w2h), (hh, w2l), (hl, w2h)):
                        last = pe.matmul(yps[j // 2][:, (j % 2) * D:(j % 2 + 1) * D], ht[C % 4][:, j * P:(j + 1) * P], wt[:, m, :],
                                         start=(m == 0 and j % 2 == 0 and ht is hh and wt is w2h), stop=(m == HC - 1 and ht is hl),
                                         skip_group_check=True)
                last.then_inc(l2_done, 1)

            def body(T):
                C = (T - 4) * 2
                if is_chunk(C - 2):
                    layer2(C - 2)
                if is_chunk(C):
                    if C % HC == 0:
                        n = T if (T.coef or T.const < 52) else Step(NT)
                        pe.wait_ge(loT_done, nth(n))
                    layer1(C)
                if is_tile(T):
                    pe.wait_ge(out2_done, nth(T + 1))
                    pe.wait_ge(outs_done, nth(T + 1))
                    pe.wait_ge(loT_done, nth(T))
                    for c in range(KC):
                        pe.transpose(tps[:, c * P:(c + 1) * P], cat[T % 2][:, c * P:(c + 1) * P], ident[:, :])
                    pe.transpose(tpr[0:3 * KR, 0:P], cat[T % 2][:, KC * P:CAT], ident[:, :]).then_inc(trans_done, 1)
                if is_chunk(C - 1):
                    layer2(C - 1)
                if is_chunk(C + 1):
                    layer1(C + 1)
                A = T + 1
                if is_tile(A):
                    pe.wait_ge(oh_done, nth(A + 1))
                    pe.wait_ge(nat_in[A % 2], nth((A // 2) * 16 + 16))
                    pe.wait_ge(outs_done, nth(A - 1))
                    for j in range(NJ):
                        last = pe.matmul(sps[A % 2][:, 0:F], onehot[A % 2][:, j, :], nat[A % 2][:, j, :], start=(j == 0), stop=(j == NJ - 1))
                    last.then_inc(sums_done, 1)
            steps(pe, body)

        @block.vector
        def _(dve):
            set_step = itertools.count(1)
            V = dve
            V.sem_inc(x_used, 1)
            V.sem_inc(g_used, 1)
            dve.wait_ge(consts, 9)
            V.tensor_scalar(out=ident[:, :], in0=iota[:, :], scalar1=pid[:, 0:1], scalar2=None, op0=ALU.is_equal).then_inc(dve_set, 1)
            dve.wait_ge(dve_set, next(set_step))
            V.tensor_scalar(out=small[1][:, 0:1], in0=pid[:, :], scalar1=1.0, scalar2=None, op0=ALU.add).then_inc(dve_set, 1)
            dve.wait_ge(dve_set, next(set_step))
            V.tensor_scalar(out=trisb[:, :], in0=iota[0:NTP, 0:NTP], scalar1=pid[0:NTP, 0:1], scalar2=None, op0=ALU.is_gt).then_inc(dve_set, 1)
            dve.wait_ge(dve_set, next(set_step))
            V.tensor_scalar(out=shift[:, :], in0=iota[0:NTP, 0:NTP], scalar1=small[1][0:NTP, 0:1], scalar2=None, op0=ALU.is_equal).then_inc(dve_set, 1)
            dve.wait_ge(dve_set, next(set_step))
            dve.wait_ge(f_in, 16)
            V.tensor_copy(ff, fi).then_inc(f_row, 1)
            dve.wait_ge(f_ps, 1)
            V.tensor_copy(fb, tps[:, 0:NROW]).then_inc(dve_set, 1)
            dve.wait_ge(dve_set, next(set_step))
            V.tensor_scalar(out=nidh[:, :], in0=nid, scalar1=0.5, scalar2=None, op0=ALU.add).then_inc(nid_half, 1)
            for t in range(NTP):
                if t % 2 == 0:
                    dve.wait_ge(cnt1_done, nth(t // 2 - 1))
                    V.tensor_scalar(out=junk[t // 2 % 2][:, 0:NROW], in0=fb, scalar1=nid[:, t:t + 1], scalar2=0.0, op0=ALU.is_le, op1=ALU.add,
                                    accum_out=cnt1[:, t:t + 1]).then_inc(cnt1_done, 1)
                if t % 10 == 9 or t == NTP - 1:
                    g = slice(t - t % 10, t + 1)
                    odd = slice(t - t % 10 + 1, t + 1, 2)
                    dve.wait_ge(cnt1_done, t // 2 + 1)
                    dve.wait_ge(cnt1_act, (t + 1) // 2)
                    V.tensor_scalar(out=cnt1[:, odd], in0=cnt1[:, odd], scalar1=0.5, scalar2=NROW / 2, op0=ALU.mult, op1=ALU.add).then_inc(dve_set, 1)
                    dve.wait_ge(dve_set, next(set_step))
                    V.tensor_scalar(out=small[2][:, g], in0=cnt1[:, g], scalar1=1.0, scalar2=-1.0, op0=ALU.max, op1=ALU.add).then_inc(dve_set, 1)
                    dve.wait_ge(dve_set, next(set_step))
                    V.tensor_copy(rowi[:, g], small[2][:, g]).then_inc(row_done, 1)
            done = 0
            steps_before = next(set_step)
            V.sem_inc(dve_set, 1)
            for t in range(NTP):
                if t % 2 == 0:
                    dve.wait_ge(rowbuf_in[t % 4], 16 * (t // 4 + 1))
                    dve.wait_ge(rowbuf_used, nth(t // 2 - 1))
                    V.tensor_scalar(out=junk[t // 2 % 2], in0=rows[t % 4], scalar1=nid[:, t:t + 1], scalar2=0.0, op0=ALU.is_le, op1=ALU.add,
                                    accum_out=cnt2[:, t:t + 1]).then_inc(rowbuf_used, 1)
                while done < min(NT, (t + 1) * NT // (NTP - 8)):
                    g = done // XG
                    if done % XG == 0:
                        dve.wait_ge(xs_in[g % 2], 16 * (g // 2 + 1) + (16 if g == XGF - 1 else 0))
                    V.bn_stats(out=stats[:, done, :], in_=xs[g % 2][:, done % XG, :]).then_inc(xs_used, 1)
                    done += 1
                    if done % XG == 0:
                        dve.wait_ge(xs_used, done)
                        for q in range(done - XG, done):
                            V.bn_aggr(out=mv[:, q, :], in_=stats[:, q, :]).then_inc(dve_set, 1)
                            next(set_step)
                if t == NTP - 7:
                    dve.wait_ge(dve_set, XG * XGF + steps_before)
                    V.tensor_scalar(out=small[8][:, 0:NT], in0=mv[:, 0:NT, 1], scalar1=EPS, scalar2=None, op0=ALU.add).then_inc(var_ready, 1)
            dve.wait_ge(rowbuf_used, (NTP + 1) // 2)
            dve.wait_ge(rowbuf_act, NTP // 2)
            V.tensor_scalar(out=cnt2[:, 1::2], in0=cnt2[:, 1::2], scalar1=0.5, scalar2=ROW / 2, op0=ALU.mult, op1=ALU.add).then_inc(dve_set, 1)
            dve.wait_ge(dve_set, next(set_step))
            V.scalar_tensor_tensor(out=small[0][:, :], in0=small[2][:, :], scalar=float(ROW), in1=cnt2[:, :], op0=ALU.mult, op1=ALU.add).then_inc(ends_ready, 1)
            dve.wait_ge(pe_set, 1)
            V.tensor_copy(et[:, :], sps[0][0:NTP, 0:P]).then_inc(et_ready, 1)
            dve.wait_ge(et_ready, 1)
            V.tensor_copy(st[:, 1:P], et[:, 0:P - 1]).then_inc(dve_set, 1)
            dve.wait_ge(dve_set, next(set_step))
            dve.wait_ge(pe_set, 3)
            V.tensor_copy(st[:, 0:1], sps[1][0:NTP, 0:1]).then_inc(st_ready, 1)
            V.tensor_scalar(out=small[1][0:1, :], in0=l1ps[0][0:1, 0:NTP], scalar1=float(NE - CAPE), scalar2=None, op0=ALU.min).then_inc(dve_set, 1)
            dve.wait_ge(dve_set, next(set_step))
            V.tensor_copy(e0row[:, :], small[1][0:1, :]).then_inc(e0_ready, 1)
            dve.wait_ge(pe_set, 4)
            E, B = small[0], small[3]
            V.tensor_copy(B[:, :], l1ps[1][:, 0:NTP]).then_inc(dve_set, 1)
            dve.wait_ge(dve_set, next(set_step))
            V.tensor_tensor(out=Dg[:, :], in0=E[:, :], in1=B[:, :], op=ALU.subtract).then_inc(dcol_ready, 1)
            dve.wait_ge(dcol_ready, 1)
            dve.wait_ge(pe_set, 5)
            V.tensor_reduce(out=dm[:, 0:1], in_=sps[0][0:NTP, 0:P], axis=AX.X, op=ALU.max).then_inc(dve_set, 1)
            dve.wait_ge(dve_set, next(set_step))
            V.memset(dm[:, 1:2], 0.0).then_inc(dve_set, 1)
            dve.wait_ge(dve_set, next(set_step))
            for q in range(XR):
                V.scalar_tensor_tensor(out=dm[:, 1:2], in0=dm[:, 0:1], scalar=float(2 * WIN + q * XW), in1=dm[:, 1:2], op0=ALU.is_gt, op1=ALU.add).then_inc(dve_set, 1)
                dve.wait_ge(dve_set, next(set_step))
            V.tensor_scalar(out=dm[:, 4:5], in0=et[:, P - 1:P], scalar1=float(NE - WIN), scalar2=None, op0=ALU.is_gt).then_inc(dve_set, 1)
            dve.wait_ge(dve_set, next(set_step))
            V.tensor_tensor(out=dm[:, 5:6], in0=dm[:, 1:2], in1=dm[:, 4:5], op=ALU.add).then_inc(dve_set, 1)
            dve.wait_ge(dve_set, next(set_step))
            V.tensor_scalar(out=dm[:, 2:3], in0=st[:, 0:1], scalar1=float(NE - CAPE), scalar2=float(CAPE), op0=ALU.min, op1=ALU.add).then_inc(dve_set, 1)
            dve.wait_ge(dve_set, next(set_step))
            V.tensor_tensor(out=dm[:, 3:4], in0=et[:, P - 1:P], in1=dm[:, 2:3], op=ALU.is_gt).then_inc(dve_set, 1)
            dve.wait_ge(dve_set, next(set_step))
            V.scalar_tensor_tensor(out=bad[0:NTP, 0:1], in0=dm[:, 0:1], scalar=float(2 * WIN + XR * XW), in1=dm[:, 3:4], op0=ALU.is_gt, op1=ALU.add).then_inc(dve_set, 1)
            dve.wait_ge(dve_set, next(set_step))
            dve.wait_ge(sd_in, 32)
            V.tensor_tensor(out=sbad[0:SR, :], in0=sd[0:SR, 0:SC], in1=sd[0:SR, 1:SC + 1], op=ALU.is_gt).then_inc(dve_set, 1)
            dve.wait_ge(dve_set, next(set_step))
            V.tensor_reduce(out=bad[0:SR, 1:2], in_=sbad[0:SR, :], axis=AX.X, op=ALU.max).then_inc(dcol_ready, 1)
            dve.wait_ge(pe_set, 6)
            V.tensor_copy(rcum[:, 0, :], l1ps[0][0:1, 0:NTP]).then_inc(dve_set, 1)
            dve.wait_ge(dve_set, next(set_step))
            V.tensor_copy(rcum[:, 2, :], l1ps[0][0:1, 64:64 + NTP]).then_inc(dve_set, 1)
            dve.wait_ge(dve_set, next(set_step))
            V.tensor_copy(rcum[:, 3, :], l1ps[0][0:1, 128:128 + NTP]).then_inc(dve_set, 1)
            dve.wait_ge(dve_set, next(set_step))
            V.tensor_copy(rcum[:, 1, :], sps[1][0:1, 0:NTP]).then_inc(dve_set, 1)
            dve.wait_ge(dve_set, next(set_step))
            V.tensor_copy(bad[0:1, :], sps[0][0:1, 0:2]).then_inc(dve_set, 1)
            dve.wait_ge(dve_set, next(set_step))
            V.tensor_tensor(out=bad[0:1, 0:1], in0=bad[0:1, 0:1], in1=bad[0:1, 1:2], op=ALU.add).then_inc(dve_set, 1)
            dve.wait_ge(dve_set, next(set_step))
            V.tensor_scalar(out=flag[:, :], in0=bad[0:1, 0:1], scalar1=0.5, scalar2=None, op0=ALU.is_gt).then_inc(flag_ready, 1)
            V.tensor_copy(tab[:, :, M_S], B[:, :]).then_inc(dve_set, 1)
            dve.wait_ge(dve_set, next(set_step))
            V.tensor_scalar(out=tab[:, :, M_E8], in0=E[:, :], scalar1=float(-XW), scalar2=None, op0=ALU.add).then_inc(dve_set, 1)
            dve.wait_ge(dve_set, next(set_step))
            V.tensor_scalar(out=tab[:, :, M_ANY], in0=Dg[:, :], scalar1=1.0, scalar2=None, op0=ALU.min).then_inc(dve_set, 1)
            dve.wait_ge(dve_set, next(set_step))
            V.tensor_scalar(out=small[5][:, :], in0=Dg[:, :], scalar1=1.0, scalar2=None, op0=ALU.max).then_inc(dve_set, 1)
            dve.wait_ge(dve_set, next(set_step))
            V.reciprocal(tab[:, :, M_RCNT], small[5][:, :]).then_inc(dve_set, 1)
            dve.wait_ge(dve_set, next(set_step))
            lev = [tab[:, :, M_B + i] for i in range(4)]
            for i in range(4):
                V.tensor_scalar(out=lev[i], in0=Dg[:, :], scalar1=float(WIN >> i), scalar2=None, op0=ALU.is_ge).then_inc(dve_set, 1)
                dve.wait_ge(dve_set, next(set_step))
            W2nd, tr = small[6], small[5]
            V.tensor_scalar(out=W2nd[:, :], in0=E[:, :], scalar1=-1.0, scalar2=None, op0=ALU.add).then_inc(dve_set, 1)
            dve.wait_ge(dve_set, next(set_step))
            for i in range(4):
                V.scalar_tensor_tensor(out=W2nd[:, :], in0=lev[i], scalar=float(-(WIN >> (i + 1))), in1=W2nd[:, :], op0=ALU.mult, op1=ALU.add).then_inc(dve_set, 1)
                dve.wait_ge(dve_set, next(set_step))
            V.tensor_scalar(out=tr[:, :], in0=W2nd[:, :], scalar1=float(NE - WIN), scalar2=None, op0=ALU.is_gt).then_inc(dve_set, 1)
            dve.wait_ge(dve_set, next(set_step))
            for i in range(4):
                V.tensor_tensor(out=lev[i], in0=lev[i], in1=tr[:, :], op=ALU.max).then_inc(dve_set, 1)
                dve.wait_ge(dve_set, next(set_step))
                V.tensor_scalar(out=lev[i], in0=lev[i], scalar1=2.0, scalar2=-1.0, op0=ALU.mult, op1=ALU.add).then_inc(dve_set, 1)
                dve.wait_ge(dve_set, next(set_step))
            V.tensor_scalar(out=tab[:, :, M_B:M_B + 4], in0=tab[:, :, M_B:M_B + 4], scalar1=FMAX, scalar2=None, op0=ALU.mult).then_inc(dve_set, 1)
            dve.wait_ge(dve_set, next(set_step))
            V.tensor_scalar(out=tab[:, :, M_XB], in0=Dg[:, :], scalar1=float(2 * WIN), scalar2=2.0, op0=ALU.is_gt, op1=ALU.mult).then_inc(dve_set, 1)
            dve.wait_ge(dve_set, next(set_step))
            V.tensor_scalar(out=tab[:, :, M_XB], in0=tab[:, :, M_XB], scalar1=-1.0, scalar2=FMAX, op0=ALU.add, op1=ALU.mult).then_inc(dve_set, 1)
            dve.wait_ge(dve_set, next(set_step))
            starts = [small[1], small[6]]
            V.tensor_scalar(out=starts[0][:, :], in0=B[:, :], scalar1=float(NE - WIN), scalar2=None, op0=ALU.min).then_inc(dve_set, 1)
            dve.wait_ge(dve_set, next(set_step))
            V.tensor_scalar(out=starts[1][:, :], in0=W2nd[:, :], scalar1=float(NE - WIN), scalar2=0.0, op0=ALU.min, op1=ALU.max).then_inc(dve_set, 1)
            dve.wait_ge(dve_set, next(set_step))
            for w in range(2):
                V.tensor_copy(tabi[:, :, w], starts[w][:, :]).then_inc(dve_set, 1)
                dve.wait_ge(dve_set, next(set_step))
                lo_, hi_ = tab[:, :, M_LO + w], tab[:, :, M_HI + w]
                V.tensor_tensor(out=lo_, in0=B[:, :], in1=starts[w][:, :], op=ALU.subtract).then_inc(dve_set, 1)
                dve.wait_ge(dve_set, next(set_step))
                V.tensor_tensor(out=lo_, in0=lo_, in1=tr[:, :], op=ALU.mult).then_inc(dve_set, 1)
                dve.wait_ge(dve_set, next(set_step))
                V.tensor_tensor(out=starts[w][:, :], in0=E[:, :], in1=starts[w][:, :], op=ALU.subtract).then_inc(dve_set, 1)
                dve.wait_ge(dve_set, next(set_step))
                V.tensor_scalar(out=hi_, in0=tr[:, :], scalar1=float(-WIN), scalar2=float(WIN), op0=ALU.mult, op1=ALU.add).then_inc(dve_set, 1)
                dve.wait_ge(dve_set, next(set_step))
                V.tensor_tensor(out=hi_, in0=hi_, in1=starts[w][:, :], op=ALU.max).then_inc(dve_set, 1)
                dve.wait_ge(dve_set, next(set_step))
            dve.wait_ge(std_ready, 1)
            r0, a, v = small[2][:, 0:NT], small[5][:, 0:NT], small[8][:, 0:NT]
            V.reciprocal(r0, small[7][:, 0:NT]).then_inc(dve_set, 1)
            dve.wait_ge(dve_set, next(set_step))
            V.tensor_tensor(out=a, in0=r0, in1=r0, op=ALU.mult).then_inc(dve_set, 1)
            dve.wait_ge(dve_set, next(set_step))
            V.tensor_tensor(out=a, in0=a, in1=v, op=ALU.mult).then_inc(dve_set, 1)
            dve.wait_ge(dve_set, next(set_step))
            V.tensor_scalar(out=a, in0=a, scalar1=-0.5, scalar2=1.5, op0=ALU.mult, op1=ALU.add).then_inc(dve_set, 1)
            dve.wait_ge(dve_set, next(set_step))
            V.memset(tab[:, NT:NTP, M_RSTD:M_OFF + 1], 0.0).then_inc(dve_set, 1)
            dve.wait_ge(dve_set, next(set_step))
            V.tensor_tensor(out=tab[:, 0:NT, M_RSTD], in0=r0, in1=a, op=ALU.mult).then_inc(dve_set, 1)
            dve.wait_ge(dve_set, next(set_step))
            V.scalar_tensor_tensor(out=tab[:, 0:NT, M_OFF], in0=mv[:, 0:NT, 0], scalar=-1.0, in1=tab[:, 0:NT, M_RSTD], op0=ALU.mult, op1=ALU.mult).then_inc(dve_set, 1)
            dve.wait_ge(dve_set, next(set_step))
            dve.wait_ge(pe_set, 7)
            V.tensor_tensor(out=b1e[:, :], in0=tpr[:, 0:HC], in1=b1c[:, :], op=ALU.add).then_inc(dve_set, 1)
            dve.wait_ge(dve_set, next(set_step))
            dve.wait_ge(pool_set, KC // 2 + 3)
            V.sem_inc(setup_free, 1)
            dve.wait_ge(setup_free, 1)
            dve.wait_ge(flag_ready, 1)
            general = dve.value_load(flag[0:1, 0:1], min_val=0, max_val=1)
            with dve.If(general > 0):
                V.memset(sumT[0:F + 1, :], 0.0).then_inc(g_upd, 1)
                V.memset(maxT[0:F, :], -FMAX).then_inc(g_upd, 1)
                V.memset(eT[F:F + 1, :], 1.0).then_inc(g_upd, 1)
                with dve.Fori(0, NROW) as r:
                    dve.wait_ge(g_in, r * 32 + 32)
                    V.sem_inc(dve_turn, 1)
                    with dve.Fori(0, ROW) as j:
                        n = dve.value_load(gdst[0:1, bass.ds(j, 1)], min_val=0, max_val=N - 1)
                        V.drain()
                        V.tensor_tensor(out=sumT[0:F + 1, bass.ds(n, 1)], in0=sumT[0:F + 1, bass.ds(n, 1)], in1=eT[0:F + 1, bass.ds(j, 1)], op=ALU.add)
                        V.tensor_tensor(out=maxT[0:F, bass.ds(n, 1)], in0=maxT[0:F, bass.ds(n, 1)], in1=eT[0:F, bass.ds(j, 1)], op=ALU.max)
                    V.drain()
                    V.sem_inc(g_used, 1)
                V.sem_inc(g_done, 1)
                dve.wait_ge(gc_in, 32)
                V.tensor_scalar(out=small[5][:, :], in0=tab[:, :, M_ANY], scalar1=1.0, scalar2=None, op0=ALU.max).then_inc(g_upd, 1)
                dve.wait_ge(g_upd, 4)
                V.reciprocal(tab[:, :, M_RCNT], small[5][:, :]).then_inc(g_upd, 1)
                V.tensor_scalar(out=tab[:, :, M_ANY], in0=tab[:, :, M_ANY], scalar1=1.0, scalar2=None, op0=ALU.min).then_inc(g_upd, 1)
                dve.wait_ge(g_upd, 6)
            V.sem_inc(setup_free, 1)

            def level(M, e, s, i):
                h = WIN >> (i + 1)
                w = e.rearrange("p (w j) f -> p w (j f)", w=2)
                V.scalar_tensor_tensor(out=w[:, :, 0:h * F], in0=w[:, :, h * F:2 * h * F], scalar=s[:, M_B + i:M_B + i + 1],
                                       in1=w[:, :, 0:h * F], op0=ALU.min, op1=ALU.max).then_inc(levels, 1)

            def lo(C):
                cols = columns(C)
                dve.wait_ge(hi_done, nth((C + 1) * 2))
                dve.wait_ge(l2_done, nth(C - 3))
                V.tensor_tensor(out=hl[C % 4][:, 0:cols], in0=hf[C % 2][:, 0:cols], in1=hh[C % 4][:, 0:cols], op=ALU.subtract).then_inc(lo_done, 1)

            def body(T):
                A = T + 2
                if is_tile(A):
                    dve.wait_ge(ndst_in[A % 4], nth((A // 4) * 16 + 16))
                    dve.wait_ge(stg_done, nth(A * 2 + 2))
                    dve.wait_ge(oh_done, nth(A))
                    V.tensor_scalar(out=dloc[:, :], in0=ndst[A % 4][:, :], scalar1=stg[A % 4][:, M_BASE:M_BASE + 1], scalar2=None, op0=ALU.subtract).then_inc(dloc_done, 1)
                    dve.wait_ge(dloc_done, nth(A + 1))
                    dve.wait_ge(sums_done, nth(A - 1))
                    V.tensor_tensor(out=onehot[A % 2][:, :, :], in0=iota[:, None, :].broadcast_to([P, NJ, P]),
                                    in1=dloc[:, :, None].broadcast_to([P, NJ, P]), op=ALU.is_equal).then_inc(oh_done, 1)
                M = T + 1
                e = ell[M % 2]
                s = stg[M % 4]
                if is_tile(M):
                    dve.wait_ge(ell_in[M % 2], nth((M // 2) * 32 + 32))
                    dve.wait_ge(stg_done, nth(M * 2 + 2))
                    extra = dve.value_load(rcum[0:1, 3, bass.ds(M.value, 1)], min_val=0, max_val=XR + 1)
                    with dve.If(extra > 0):
                        past = dve.value_load(rcum[0:1, 2, bass.ds(M.value, 1)], min_val=0, max_val=1)
                        with dve.If(past > 0):
                            dve.wait_ge(out2_done, nth(M))
                            V.sem_inc(masked, 1)
                            for w in range(2):
                                V.tensor_scalar(out=wmask[:, w, :], in0=iota16[:, :], scalar1=s[:, M_LO + w:M_LO + w + 1], scalar2=None, op0=ALU.is_ge)
                                V.drain()
                                V.scalar_tensor_tensor(out=wmask[:, w, :], in0=iota16[:, :], scalar=s[:, M_HI + w:M_HI + w + 1], in1=wmask[:, w, :], op0=ALU.is_lt, op1=ALU.mult)
                                V.drain()
                            V.tensor_scalar(out=wmask[:, :, :], in0=wmask[:, :, :], scalar1=2.0, scalar2=-1.0, op0=ALU.mult, op1=ALU.add)
                            V.drain()
                            V.tensor_scalar(out=wmask[:, :, :], in0=wmask[:, :, :], scalar1=FMAX, scalar2=None, op0=ALU.mult)
                            V.drain()
                            V.tensor_tensor(out=e[:, :, :], in0=e[:, :, :], in1=wmask[:, :, :].rearrange("p w j -> p (w j)")[:, :, None].broadcast_to([P, 2 * WIN, F]), op=ALU.min)
                            V.drain()
                        rounds = dve.value_load(rcum[0:1, 0, bass.ds(M.value, 1)], min_val=0, max_val=XR)
                        with dve.If(rounds > 0):
                            before = dve.value_load(rcum[0:1, 1, bass.ds(M.value, 1)], min_val=0, max_val=XR * NTP)
                            with dve.Fori(0, rounds) as q:
                                dve.wait_ge(x_in_w, (before + q) * 16 + 16)
                                V.tensor_reduce(out=mxx[:, :], in_=xw.rearrange("p (j f) -> p f j", f=F), axis=AX.X, op=ALU.max).then_inc(x_red, 1)
                                dve.wait_ge(x_red, before + q + 1)
                                V.scalar_tensor_tensor(out=e[:, 0, :], in0=mxx[:, :], scalar=s[:, M_XB:M_XB + 1], in1=e[:, 0, :], op0=ALU.min, op1=ALU.max).then_inc(x_used, 1)
                                dve.wait_ge(x_used, before + q + 2)
                                V.sem_inc(dve_turn, 1)
                    level(M, e, s, 0)
                C = (T - 4) * 2
                if is_chunk(C):
                    lo(C)
                if is_tile(T):
                    b, k = (T // 4) % 2, T % 4
                    ks = slice(k * P, (k + 1) * P)
                    dve.wait_ge(hiT_done, nth(T * 2 + 2))
                    V.tensor_tensor(out=inl[b][:, :, ks], in0=tps[:, :].rearrange("p (c n) -> p c n", n=P), in1=inh[b][:, :, ks], op=ALU.subtract)
                    V.tensor_tensor(out=inr[b][2 * KR:3 * KR, ks], in0=tpr[2 * KR:3 * KR, 0:P], in1=inr[b][2 * KR:3 * KR, ks], op=ALU.subtract).then_inc(loT_done, 1)
                if is_tile(M):
                    for i in range(1, 4):
                        dve.wait_ge(levels, nth(M * 4 + i))
                        level(M, e, s, i)
                    dve.wait_ge(levels, nth(M * 4 + 4))
                    V.tensor_tensor(out=e[:, 0, :], in0=e[:, 0, :], in1=e[:, WIN, :], op=ALU.max).then_inc(max2, 1)
                    dve.wait_ge(max2, nth(M + 1))
                    dve.wait_ge(trans_done, nth(M - 1))
                    V.tensor_scalar(out=cat[M % 2][:, D + F:D + 2 * F], in0=e[:, 0, :], scalar1=s[:, M_ANY:M_ANY + 1], scalar2=None, op0=ALU.mult).then_inc(gmix, 1)
                    dve.wait_ge(gmix, nth(M + 1))
                    V.sem_inc(dve_turn, 1)
                    with dve.If(general > 0):
                        dve.wait_ge(outs_done, nth(M + 1))
                        dve.wait_ge(gt_in, nth(M * 32 + 32))
                        c = cat[M % 2]
                        rc = s[:, M_RCNT:M_RCNT + 1]
                        V.tensor_copy(c[:, D:D + F], gst[:, 0, :])
                        V.tensor_scalar(out=c[:, D + F:D + 2 * F], in0=gst[:, 1, :], scalar1=s[:, M_ANY:M_ANY + 1], scalar2=None, op0=ALU.mult)
                        V.tensor_scalar(out=c[:, D + 2 * F:KC * P], in0=gst[:, 0, 0:F - KR], scalar1=rc, scalar2=None, op0=ALU.mult)
                        V.tensor_scalar(out=c[:, KC * P:CAT].rearrange("p (r k) -> p r k", k=KR), in0=gst[:, 0, None, F - KR:F].broadcast_to([P, 3, KR]),
                                        scalar1=rc, scalar2=None, op0=ALU.mult).then_inc(gt_used, 1)
                        dve.wait_ge(gt_used, nth(M + 1))
                        V.sem_inc(dve_turn, 1)
                    V.sem_inc(out2_done, 1)
                if is_chunk(C + 1):
                    lo(C + 1)
            steps(dve, body)


_INS = ["x", "dst", "edge_attr_96", "L0_gnn_u", "L0_gnn_W1", "L0_gnn_b1", "L0_gnn_W2", "L0_gnn_b2"]


def kernel(**inputs):
    import numpy as _np
    import concourse.bacc as _bacc
    from concourse import mybir as _mybir
    from concourse.bass_utils import run_bass_kernel_spmd as _run

    nc = _bacc.Bacc("TRN2", target_bir_lowering=False, num_devices=1)
    arrays, args = {}, []
    for name in _INS:
        a = _np.ascontiguousarray(inputs[name])
        arrays[f"in_{name}"] = a
        args.append(nc.dram_tensor(f"in_{name}", a.shape, _mybir.dt.from_np(a.dtype), kind="ExternalInput").ap())
    shape = inputs["x"].shape
    args.append(nc.dram_tensor("out_y", shape, _mybir.dt.float32, kind="ExternalOutput").ap())
    gnn_block(nc, *args)
    r = _run(nc, [arrays], core_ids=[0])
    return r.results[0]["out_y"]
```

```python
import itertools

import concourse.bass as bass
from concourse import mybir

P = 128


class Step:

    def __init__(self, const, coef=0, reg=None):
        self.const, self.coef, self.reg = const, coef, reg

    def __add__(self, n):
        return Step(self.const + n, self.coef, self.reg)

    def __sub__(self, n):
        return self + (-n)

    def __mul__(self, n):
        return Step(self.const * n, self.coef * n, self.reg)

    def __floordiv__(self, n):
        assert self.coef % n == 0
        return Step(self.const // n, self.coef // n, self.reg)

    def __mod__(self, n):
        assert self.coef % n == 0
        return self.const % n

    @property
    def value(self):
        return self.const if not self.coef else self.reg * self.coef + self.const


def nth(count):
    if isinstance(count, Step):
        if count.coef:
            assert count.const > 0
            return count.value
        count = count.const
    return max(count, 0)


def gnn_block(nc, x, dst, edge, u, W1, b1, W2, b2, out):
    f32, f32r, i32 = mybir.dt.float32, mybir.dt.float32r, mybir.dt.int32
    ALU, ACT, AX = mybir.AluOpType, mybir.ActivationFunctionType, mybir.AxisListType

    N, D = x.shape
    NE, F = edge.shape
    G = u.shape[1]
    H = W1.shape[1]
    NT = -(-N // P)
    NTP = NT + 1
    BT = 4
    NB = -(-NT // BT)
    HC = H // P
    K = D + 3 * F
    assert K + G == W1.shape[0]
    KC = K // P
    KR = K - KC * P
    CAT = KC * P + 3 * KR
    NJ = 19
    CAPE = NJ * P
    WIN = 16
    XW = 8
    XR = 8
    ROW = 250
    NROW = NE // ROW
    assert NROW * ROW == NE
    LAST = N - (NT - 1) * P
    FMAX = 3.3895e38
    EPS = 1e-5

    sb = {}

    def sbuf(name, shape, dt=f32):
        sb[name] = nc.alloc_sbuf_tensor(name, shape, dt)
        return sb[name]

    w1h, w1l = sbuf("w1h", [P, KC, H], f32r), sbuf("w1l", [P, KC, H], f32r)
    w1r = sbuf("w1r", [3 * KR, H], f32r)
    w2h, w2l = sbuf("w2h", [P, HC, D], f32r), sbuf("w2l", [P, HC, D], f32r)
    b1e, b2b = sbuf("b1e", [P, HC]), sbuf("b2b", [P, D])
    inh = [sbuf(f"inh{i}", [P, KC, BT * P], f32r) for i in range(2)]
    inl = [sbuf(f"inl{i}", [P, KC, BT * P], f32r) for i in range(2)]
    inr = [sbuf(f"inr{i}", [3 * KR, BT * P], f32r) for i in range(2)]
    hf = [sbuf(f"hf{i}", [P, BT * P]) for i in range(2)]
    hh = [sbuf(f"hh{i}", [P, BT * P], f32r) for i in range(2)]
    hl = [sbuf(f"hl{i}", [P, BT * P], f32r) for i in range(2)]
    natn, elln = NJ * F, 2 * WIN * F
    GROUPS = [0, *range(4, NTP, 6), NTP]
    LAG = 12
    work = sbuf("work", [P, 2 * (natn + elln)])
    natf = [work[:, i * natn:(i + 1) * natn] for i in range(2)]
    nat = [t.rearrange("p (j f) -> p j f", f=F) for t in natf]
    onehot = [sbuf(f"onehot{i}", [P, NJ, P], f32r) for i in range(2)]
    ellf = [work[:, 2 * natn + i * elln:2 * natn + (i + 1) * elln] for i in range(2)]
    ell = [t.rearrange("p (j f) -> p j f", f=F) for t in ellf]
    ndst = [sbuf(f"ndst{i}", [P, NJ], i32) for i in range(4)]
    nhl = sbuf("nhl", [P, NJ, 2 * F], f32r)
    nath, natl = nhl[:, :, 0:F], nhl[:, :, F:2 * F]
    JD = 5
    dloc = sbuf("dloc", [P, NJ])
    mxx = sbuf("mxx", [P, F])
    wmask = sbuf("wmask", [P, 2, WIN])
    cat = [sbuf(f"cat{i}", [P, CAT]) for i in range(2)]
    xin = [sbuf(f"xin{i}", [P, D]) for i in range(2)]
    xball = sbuf("xb", [P, 8 * D])
    xb = [xball[:, i * D:(i + 1) * D] for i in range(8)]
    yc = sbuf("yc", [P, 4, D])
    yo = sbuf("yo", [P, 4, D])
    M_B, M_XB, M_ANY, M_RCNT, M_BASE, M_RSTD, M_OFF, M_S, M_E8, M_LO, M_HI, NM = 0, 4, 5, 6, 7, 8, 9, 10, 11, 12, 14, 16
    tab = sbuf("tab", [P, NTP, NM])
    tabi = sbuf("tabi", [P, NTP, 2], i32)
    stg = [sbuf(f"stg{i}", [P, NM]) for i in range(4)]
    stgi = [sbuf(f"stgi{i}", [P, 2], i32) for i in range(4)]
    ident = sbuf("ident", [P, P])
    iota = sbuf("iota", [P, P])
    e0row = sbuf("e0row", [1, NTP], i32)
    rawf = [t[:, 0:2 * H] for t in ellf]
    scratch = sbuf("scratch", [P, 20 * NTP])
    cols = [scratch[:, i * NTP:(i + 1) * NTP] for i in range(20)]
    nid, cnt1, cnt2, rowi = cols[0], cols[1], cols[2], cols[3].bitcast(i32)
    RB = 8
    rows = [natf[1][:, i * ROW:(i + 1) * ROW].bitcast(i32) for i in range(RB - 1)]
    rows.append(natf[0][:, H + NROW:H + NROW + ROW].bitcast(i32))
    hfw = [yc[:, :, :], yo[:, :, :]]
    small = cols[4:13]
    Dg = small[4]
    stats = scratch[:, 13 * NTP:13 * NTP + 6 * NT].rearrange("p (t s) -> p t s", s=6)
    mv = sbuf("mv", [P, NTP, 2])
    pid, pid1 = sbuf("pid", [P, 1]), sbuf("pid1", [P, 1])
    ones = sbuf("ones", [1, P])
    fi = yo[0:1, 0:2, :].rearrange("p a d -> p (a d)")[:, 0:NROW].bitcast(i32)
    ff = yo[0:1, 2:4, :].rearrange("p a d -> p (a d)")[:, 0:NROW]
    trisb = sbuf("tri", [NTP, NTP])
    rcum = sbuf("rcum", [1, 4, NTP], i32)
    flag = sbuf("flag", [1, 1], i32)
    onesc = sbuf("onesc", [P, 1])
    bad = sbuf("bad", [P, 2])
    dm = sbuf("dm", [NTP, 8])
    xi, xif = sbuf("xi", [P, 1], i32), sbuf("xif", [P, 2])
    xw = scratch[:, 0:XW * F]
    gst = scratch[:, XW * F:(XW + 2) * F].rearrange("p (a f) -> p a f", f=F)
    nodeT = work[:, 0:NT * P]
    eT = work[:, NT * P:NT * P + ROW]
    gdst = work[0:1, NT * P + ROW:NT * P + 2 * ROW].bitcast(i32)
    fb = hf[1][:, 0:NROW]
    ends = sbuf("ends", [P, NTP + 1])
    shiftn, wrapn = cat[0][:, 0:P], cat[0][:, P:2 * P]
    thr, thrj = sbuf("thr", [NTP, XR]), sbuf("thrj", [NTP, XR])
    koff = sbuf("koff", [P, XR])
    iota16 = sbuf("iota16", [P, WIN])
    u0 = sbuf("u0", [G, 1])
    w1u = ellf[0][0:G, 2 * H:3 * H]
    b1c = cat[0][:, 2 * P:2 * P + HC]
    junka = [natf[0][:, H:H + NROW], cat[1][:, 0:NROW]]
    nidh = cat[1][:, NROW:NROW + NTP]
    junk = [ellf[1][:, 2 * H:2 * H + NROW], hf[0][:, 0:NROW]]

    def psum(name, shape):
        return nc.alloc_psum_tensor(name, shape, f32)

    l1ps = [psum(f"l1ps{i}", [P, BT * P]) for i in range(2)]
    yps = [psum(f"yps{i}", [P, 2 * D]) for i in range(2)]
    tps, tpr = psum("tps", [P, BT * P]), psum("tpr", [P, BT * P])
    sps = [psum(f"sps{i}", [P, 512]) for i in range(2)]

    S = nc.alloc_semaphore
    w_in, r_in, w2_in, c_in = S("w_in"), S("r_in"), S("w2_in"), S("c_in")
    consts, f_in, f_row, f_ps, f_sb = S("consts"), S("f_in"), S("f_row"), S("f_ps"), S("f_sb")
    cnt1_done, row_done, rowbuf_used = S("cnt1_done"), S("row_done"), S("rowbuf_used")
    cnt1_act, rowbuf_act, nid_half = S("cnt1_act"), S("rowbuf_act"), S("nid_half")
    rnd_in = S("rnd_in")
    rowbuf_in = [S(f"rows_or_stores{i}") for i in range(8)]
    dve_set, pe_set, act_set, pool_set = S("dve_set"), S("pe_set"), S("act_set"), S("pool_set")
    xs_in = [S(f"xs_in{i}") for i in range(2)]
    xs_used, e0_ready, setup_free = S("xs_used"), S("e0_ready"), S("setup_free")
    var_ready, std_ready = S("var_ready"), S("std_ready")
    ends_ready, dcol_ready = S("ends_ready"), S("dcol_ready")
    nat_in = [S(f"nat_in{i}") for i in range(2)]
    ndst_in = [S(f"ndst_in{i}") for i in range(4)]
    x_in = [S(f"x_in{i}") for i in range(2)]
    ell_in = [S(f"ell_in{i}") for i in range(2)]
    dloc_done, oh_done, sums_done, trans_done = S("dloc_done"), S("oh_done"), S("sums_done"), S("trans_done")
    l1_done, l2_done = S("l1_done"), S("l2_done")
    hi_done, lo_done, hiT_done, loT_done = S("hi_done"), S("lo_done"), S("hiT_done"), S("loT_done")
    h_done, outs_done, masked, levels, max2, out2_done = (S(n) for n in
        ("h_done", "outs_done", "masked", "levels", "max2", "out2_done"))
    stg_done, xb_part, xb_done, add_done, evac_done = (S(n) for n in
        ("stg_done", "xb_part", "xb_done", "add_done", "evac_done"))
    nhi_done, nlo_dve, nlo_pool = S("nhi_done"), S("nlo_dve"), S("nlo_pool")
    lo_set, joined = S("lo_set"), S("joined")
    gmix, dve_turn = S("gmix"), S("dve_turn")
    pool_turn, sd_in, x_idx, x_in_w, x_red, x_used = (S(n) for n in ("pool_turn", "sd_in", "x_idx", "x_in_w", "x_red", "x_used"))
    flag_ready, sd_done, g_in, g_used, g_upd, g_done, g_out, gc_in, gt_in, gt_used = (S(n) for n in
        ("flag_ready", "sd_done", "g_in", "g_used", "g_upd", "g_done", "g_out", "gc_in", "gt_in", "gt_used"))
    stored = rowbuf_in[0:4]
    gathered = [16 * len(range(r, NTP, RB)) for r in range(RB)]

    edge_rows = edge
    gsum = nc.dram_tensor("gsum", [NT * P, F], f32, kind="Internal").ap()
    gmax = nc.dram_tensor("gmax", [NT * P, F], f32, kind="Internal").ap()
    gcnt = nc.dram_tensor("gcnt", [1, NT * P], f32, kind="Internal").ap()
    dst_row = dst.rearrange("(r c) -> r c", c=ROW)

    SC = 850
    SR = NE // SC
    assert SR * SC == NE and SR <= P and SC < 4 * D
    sd = xball[:, 0:SC + 1].bitcast(i32)
    sbad = xball[:, 4 * D:4 * D + SC]

    XG = 7
    XGF = NT // XG
    assert XGF * XG == NT
    xs = [ellf[i][:, 0:XG * D].rearrange("p (t d) -> p t d", d=D) for i in range(2)]

    def steps(eng, body):
        for t in range(-2, 8):
            body(Step(t))
        with eng.Fori(0, 5) as i:
            for t in range(8, 16):
                body(Step(t, 8, i))
        for t in range(48, 57):
            body(Step(t))

    def is_tile(T, n=NT):
        return bool(T.coef) or 0 <= T.const < n

    def is_chunk(C):
        return bool(C.coef) or 0 <= C.const < NC_ALL

    NC_ALL = HC * NB

    def columns(C):
        return P if (not C.coef and C.const // HC == NB - 1) else BT * P

    with nc.Block() as block:

        @block.sync
        def _(sp):
            sp.dma_start(fi, dst_row[:, 0:1].rearrange("r c -> c r"), allow_slow_non_contiguous=True).then_inc(f_in, 16)
            def load_x(g):
                sp.wait_ge(xs_used, nth((g - 1) * XG))
                full = XG if g < XGF - 1 else XG - 1
                sp.dma_start(xs[g % 2][:, 0:full, :],
                             x[g * XG * P:(g * XG + full) * P, :].rearrange("(t p) d -> p t d", p=P)).then_inc(xs_in[g % 2], 16)
                if full < XG:
                    sp.dma_start(xs[g % 2][0:LAST, full, :], x[(NT - 1) * P:N, :]).then_inc(xs_in[g % 2], 16)
            sp.dma_start(sd[0:SR, 0:SC], dst.rearrange("(r c) -> r c", c=SC)).then_inc(sd_in, 16)
            sp.wait_ge(consts, 11)
            sp.dma_start(sd[0:SR - 1, SC:SC + 1], dst.rearrange("(r c) -> r c", c=SC)[1:SR, 0:1], allow_slow_non_contiguous=True).then_inc(sd_in, 16)
            for c in range(0, KC, 2):
                sp.dma_start(rawf[c // 2][:, 0:2 * H].rearrange("p (c h) -> p c h", h=H),
                             W1[c * P:(c + 2) * P, :].rearrange("(c p) h -> p c h", p=P)).then_inc(w_in, 16)
            for r in range(3):
                sp.dma_start(natf[0][r * KR:(r + 1) * KR, 0:H], W1[KC * P:K, :]).then_inc(r_in, 16)
            sp.wait_ge(f_ps, 1)
            for c in range(2):
                sp.dma_start(hfw[c], W2[c * 4 * P:(c + 1) * 4 * P, :].rearrange("(c p) d -> p c d", p=P)).then_inc(w2_in, 16)
            sp.dma_start(w1u, W1[K:K + G, :]).then_inc(c_in, 16)
            sp.dma_start(u0[:, :], u[0:1, :].rearrange("a g -> g a"), allow_slow_non_contiguous=True).then_inc(c_in, 16)
            sp.dma_start(b1c[:, :], b1.rearrange("(c p) -> p c", p=P), allow_slow_non_contiguous=True).then_inc(c_in, 16)
            sp.dma_start(b2b[:, :], b2.rearrange("(a d) -> a d", a=1).broadcast_to([P, D])).then_inc(c_in, 16)
            sp.wait_ge(lo_set, 3)
            sp.wait_ge(pe_set, 1)
            for g in range(XGF):
                load_x(g)
            sp.wait_ge(e0_ready, 1)
            sp.wait_ge(setup_free, 1)
            sp.wait_ge(flag_ready, 1)
            general = sp.value_load(flag[0:1, 0:1], min_val=0, max_val=1)
            with sp.If(general > 0):
                for p, gout in enumerate((gsum, gmax)):
                    with sp.Fori(0, NROW) as r:
                        sp.wait_ge(g_used, r + (p * NROW + 1))
                        sp.dma_start(gdst, dst_row[bass.ds(r, 1), :]).then_inc(g_in, 16)
                        sp.dma_start(eT[0:F, :], edge[bass.ds(r * ROW, ROW), :].rearrange("e f -> f e"), allow_slow_non_contiguous=True).then_inc(g_in, 16)
                    sp.wait_ge(g_done, p + 1)
                    sp.dma_start(gout.rearrange("n f -> f n"), nodeT[0:F, :], allow_slow_non_contiguous=True).then_inc(g_out, 16)
                    if p == 0:
                        sp.dma_start(gcnt, nodeT[F:F + 1, :]).then_inc(g_out, 16)
                    sp.wait_ge(g_out, 32 + p * 16)
                sp.dma_start(tab[:, 0:NT - 1, M_ANY], gcnt[0:1, 0:(NT - 1) * P].rearrange("a (t p) -> (a p) t", p=P), allow_slow_non_contiguous=True).then_inc(gc_in, 16)
                sp.dma_start(tab[0:LAST, NT - 1:NT, M_ANY], gcnt[0:1, (NT - 1) * P:N].rearrange("a (t p) -> (a p) t", t=1), allow_slow_non_contiguous=True).then_inc(gc_in, 16)
            sp.wait_ge(setup_free, 2)

            def body(T):
                D2 = T + 2
                if is_tile(D2, NTP):
                    sp.wait_ge(dloc_done, nth(D2 - 3))
                    first = sp.value_load(e0row[0:1, bass.ds(D2.value, 1)], min_val=0, max_val=NE - CAPE)
                    sp.dma_start(ndst[D2 % 4][:, :], dst[bass.ds(first, CAPE)].rearrange("(p j) -> p j", j=NJ)).then_inc(ndst_in[D2 % 4], 16)
                if is_tile(T):
                    first = sp.value_load(e0row[0:1, bass.ds(T.value, 1)], min_val=0, max_val=NE - CAPE)
                    sp.wait_ge(nlo_dve, nth(T - 1))
                    sp.wait_ge(nlo_pool, nth(T - 1))
                    sp.dma_start(nat[T % 2][:, :, :], edge_rows[bass.ds(first, CAPE), :].rearrange("(p j) f -> p j f", j=NJ)).then_inc(nat_in[T % 2], 16)
                    sp.wait_ge(xb_done, nth(T - 1))
                    sp.wait_ge(h_done, nth(T - 1))
                    if T.coef or T.const < NT - 1:
                        sp.dma_start(xin[T % 2][:, :], x[bass.ds(T.value * P, P), :] if T.coef else x[T.const * P:(T.const + 1) * P, :]).then_inc(x_in[T % 2], 16)
                    else:
                        sp.dma_start(xin[T % 2][0:LAST, :], x[T.const * P:N, :]).then_inc(x_in[T % 2], 16)
                G = T
                if is_tile(G):
                    with sp.If(general > 0):
                        sp.wait_ge(gt_used, nth(G))
                        n = P if (G.coef or G.const < NT - 1) else LAST
                        at = bass.ds(G.value * P, P) if G.coef else slice(G.const * P, G.const * P + n)
                        sp.dma_start(gst[0:n, 0, :], gsum[at, :]).then_inc(gt_in, 16)
                        sp.dma_start(gst[0:n, 1, :], gmax[at, :]).then_inc(gt_in, 16)
            steps(sp, body)

        @block.gpsimd
        def _(pool):
            kw = dict(allow_small_or_imprecise_dtypes=True)
            pool.sem_inc(add_done, 1)
            pool.iota(iota[:, :], pattern=[[1, P]], base=0, channel_multiplier=0, **kw).then_inc(consts, 1)
            pool.iota(pid[:, :], pattern=[[1, 1]], base=0, channel_multiplier=1, **kw).then_inc(consts, 1)
            pool.iota(nid[:, :], pattern=[[P, NTP]], base=0, channel_multiplier=1, **kw).then_inc(consts, 1)
            pool.iota(iota16[:, :], pattern=[[1, WIN]], base=0, channel_multiplier=0, **kw).then_inc(consts, 1)
            pool.iota(tab[:, :, M_BASE], pattern=[[P, NTP]], base=0, channel_multiplier=0, **kw).then_inc(consts, 1)
            pool.iota(koff[:, :], pattern=[[XW, XR]], base=WIN, channel_multiplier=0, **kw).then_inc(consts, 1)
            pool.memset(ones[:, :], 1.0).then_inc(consts, 1)
            pool.memset(sd[:, SC:SC + 1], N).then_inc(consts, 1)
            pool.memset(onesc[:, :], 1.0).then_inc(consts, 1)
            pool.memset(ends[:, 0:1], 0.0).then_inc(consts, 1)
            pool.memset(bad[:, :], 0.0).then_inc(consts, 1)
            for g in range(len(GROUPS) - 1):
                pool.wait_ge(row_done, g + 1)
                for t in range(GROUPS[g], GROUPS[g + 1]):
                    pool.wait_ge(rowbuf_act if t % 2 else rowbuf_used, nth((t - RB) // 2 + 1))
                    pool.indirect_dma_start(out=rows[t % RB], out_offset=None, in_=dst_row,
                                            in_offset=bass.IndirectOffsetOnAxis(ap=rowi[:, t:t + 1], axis=0)).then_inc(rowbuf_in[t % RB], 16)
            pool.wait_ge(setup_free, 2)

            def body(T):
                A = T + 2
                if is_tile(A, NTP):
                    pool.wait_ge(outs_done, nth(A - 3))
                    pool.wait_ge(out2_done, nth(A - 3))
                    pool.wait_ge(gmix, nth(A - 1))
                    pool.sem_inc(pool_turn, 1)
                    at = A.value
                    pool.tensor_copy(stg[A % 4][:, :], tab[:, bass.ds(at, 1), :]).then_inc(stg_done, 1)
                    pool.tensor_copy(stgi[A % 4][:, :], tabi[:, bass.ds(at, 1), :]).then_inc(stg_done, 1)
                    pool.wait_ge(stg_done, nth(A * 2 + 2))
                    pool.sem_inc(pool_turn, 1)
                    for w in range(2):
                        pool.indirect_dma_start(out=ellf[A % 2][:, w * WIN * F:(w + 1) * WIN * F], out_offset=None, in_=edge,
                                                in_offset=bass.IndirectOffsetOnAxis(ap=stgi[A % 4][:, w:w + 1], axis=0)).then_inc(ell_in[A % 2], 16)
                M = T + 1
                if is_tile(M):
                    pool.wait_ge(nhi_done, nth(M + 1))
                    pool.tensor_tensor(out=natl[:, JD:NJ, :], in0=nat[M % 2][:, JD:NJ, :], in1=nath[:, JD:NJ, :], op=ALU.subtract).then_inc(nlo_pool, 1)
                U = T - 8
                if is_tile(U):
                    rows_ = P if (U.coef or U.const < NT - 1) else LAST
                    pool.wait_ge(evac_done, nth(U + 1))
                    pool.wait_ge(stored[U % 4], nth((U // 4) * 16 + gathered[U % 4]))
                    pool.tensor_tensor(out=yo[:, U % 4, :], in0=yc[:, U % 4, :], in1=xb[U % 8][:, :], op=ALU.add).then_inc(add_done, 1)
                    pool.wait_ge(add_done, nth(U + 2))
                    pool.sem_inc(pool_turn, 1)
                    where = out[bass.ds(U.value * P, P), :] if U.coef else out[U.const * P:U.const * P + rows_, :]
                    pool.dma_start(where, yo[0:rows_, U % 4, :]).then_inc(stored[U % 4], 16)
                if is_tile(T):
                    pool.wait_ge(h_done, nth(T + 1))
                    pool.wait_ge(xb_part, nth(T))
                    pool.wait_ge(add_done, nth(T - 6))
                    pool.tensor_tensor(out=xb[T % 8][:, :], in0=xin[T % 2][:, :], in1=cat[T % 2][:, 0:D], op=ALU.add).then_inc(xb_part, 1)
                    pool.wait_ge(xb_part, nth(T + 1))
                    pool.tensor_tensor(out=xb[T % 8][:, :], in0=xb[T % 8][:, :], in1=b2b[:, :], op=ALU.add).then_inc(xb_done, 1)
                if is_tile(A, NTP):
                    rounds = pool.value_load(rcum[0:1, 0, bass.ds(at, 1)], min_val=0, max_val=XR)
                    with pool.If(rounds > 0):
                        before = pool.value_load(rcum[0:1, 1, bass.ds(at, 1)], min_val=0, max_val=XR * NTP)
                        g = stg[A % 4]
                        with pool.Fori(0, rounds) as q:
                            pool.wait_ge(x_used, before + q + 1)
                            pool.sem_inc(pool_turn, 1)
                            pool.tensor_copy(xif[:, 0:1], koff[:, bass.ds(q, 1)]).then_inc(x_idx, 1)
                            pool.wait_ge(x_idx, (before + q) * 4 + 1)
                            pool.sem_inc(pool_turn, 1)
                            pool.tensor_scalar(out=xif[:, 0:1], in0=xif[:, 0:1], scalar1=g[:, M_S:M_S + 1], scalar2=None, op0=ALU.add).then_inc(x_idx, 1)
                            pool.wait_ge(x_idx, (before + q) * 4 + 2)
                            pool.sem_inc(pool_turn, 1)
                            pool.tensor_scalar(out=xif[:, 1:2], in0=xif[:, 0:1], scalar1=g[:, M_E8:M_E8 + 1], scalar2=g[:, M_S:M_S + 1], op0=ALU.min, op1=ALU.max).then_inc(x_idx, 1)
                            pool.wait_ge(x_idx, (before + q) * 4 + 3)
                            pool.sem_inc(pool_turn, 1)
                            pool.tensor_scalar(out=xi[:, :], in0=xif[:, 1:2], scalar1=float(NE - XW), scalar2=None, op0=ALU.min).then_inc(x_idx, 1)
                            pool.wait_ge(x_idx, (before + q) * 4 + 4)
                            pool.sem_inc(pool_turn, 1)
                            pool.indirect_dma_start(out=xw, out_offset=None, in_=edge,
                                                    in_offset=bass.IndirectOffsetOnAxis(ap=xi[:, 0:1], axis=0)).then_inc(x_in_w, 16)
            pool.wait_ge(c_in, 64)
            steps(pool, body)
            for r in range(4):
                pool.wait_ge(stored[r], nth(16 * len(range(r, NT, 4)) + gathered[r]))
            for r in range(2):
                pool.wait_ge(ell_in[r], nth(32 * len(range(r, NTP, 2))))

        @block.scalar
        def _(act):
            act.wait_ge(nid_half, 1)
            act.wait_ge(f_ps, 1)
            for i in range(1, NTP + LAG):
                if i % 2 and i < NTP:
                    act.wait_ge(cnt1_act, nth(i // 2 - 1))
                    act.wait_ge(rowbuf_act, nth((i - 2 - LAG) // 2 + 1))
                    act.activation(junka[i // 2 % 2][:, 0:NROW], tps[:, 0:NROW], ACT.Sign, bias=nidh[:, i:i + 1], scale=-1.0,
                                   accum_out=cnt1[:, i:i + 1]).then_inc(cnt1_act, 1)
                if i == 10:
                    act.wait_ge(w_in, 8 * KC)
                    for c in range(0, KC, 2):
                        act.activation(w1h[:, c:c + 2, :], rawf[c // 2].rearrange("p (c h) -> p c h", h=H), ACT.Copy).then_inc(act_set, 1)
                    act.wait_ge(r_in, 48)
                    act.activation(w1r[:, :], natf[0][0:3 * KR, 0:H], ACT.Copy).then_inc(act_set, 1)
                if i == 20:
                    act.wait_ge(w2_in, 32)
                    for c in range(2):
                        act.activation(w2h[:, c * 4:(c + 1) * 4, :], hfw[c], ACT.Copy).then_inc(act_set, 1)
                t = i - LAG
                if t > 0 and t % 2:
                    act.wait_ge(rowbuf_in[t % RB], 16 * (t // RB + 1))
                    act.wait_ge(rowbuf_act, nth(t // 2 - 1))
                    act.wait_ge(cnt1_act, min(i, NTP) // 2)
                    act.activation(junka[(t // 2 + 1) % 2][:, 0:ROW], rows[t % RB], ACT.Sign, bias=nidh[:, t:t + 1], scale=-1.0,
                                   accum_out=cnt2[:, t:t + 1]).then_inc(rowbuf_act, 1)
            act.wait_ge(var_ready, 1)
            act.activation(small[7][:, 0:NT], small[8][:, 0:NT], ACT.Sqrt).then_inc(std_ready, 1)
            act.wait_ge(setup_free, 2)

            def relu(C):
                cols = columns(C)
                m = C % HC
                act.wait_ge(l1_done, nth(C + 1))
                act.wait_ge(lo_done, nth(C - 1))
                act.activation(hf[C % 2][:, 0:cols], l1ps[C % 2][:, 0:cols], ACT.Relu, bias=b1e[:, m:m + 1]).then_inc(hi_done, 1)
                act.wait_ge(l2_done, nth(C - 1))
                act.activation(hh[C % 2][:, 0:cols], l1ps[C % 2][:, 0:cols], ACT.Relu, bias=b1e[:, m:m + 1]).then_inc(hi_done, 1)

            def body(T):
                C = (T - 4) * 2
                A = T + 1
                if is_tile(A):
                    act.wait_ge(nat_in[A % 2], nth((A // 2) * 16 + 16))
                    act.wait_ge(sums_done, nth(A))
                    act.activation(nath[:, :, :], nat[A % 2][:, :, :], ACT.Copy).then_inc(nhi_done, 1)
                if is_tile(T):
                    c, sc = cat[T % 2], stg[T % 4][:, M_RCNT:M_RCNT + 1]
                    act.wait_ge(joined, nth(T + 1))
                    act.activation(c[:, D + 2 * F:KC * P], c[:, D:D + F - KR], ACT.Copy, scale=sc)
                    act.activation(c[:, KC * P:CAT].rearrange("p (r k) -> p r k", k=KR), c[:, None, D + F - KR:D + F].broadcast_to([P, 3, KR]),
                                   ACT.Copy, scale=sc).then_inc(outs_done, 1)
                if is_chunk(C):
                    relu(C)
                if is_tile(T):
                    b, k = (T // 4) % 2, T % 4
                    act.wait_ge(trans_done, nth(T + 1))
                    act.activation(inh[b][:, :, k * P:(k + 1) * P], tps[:, :].rearrange("p (c n) -> p c n", n=P), ACT.Copy).then_inc(hiT_done, 1)
                    act.activation(inr[b][:, k * P:(k + 1) * P], tpr[0:3 * KR, 0:P], ACT.Copy).then_inc(hiT_done, 1)
                A = T + 1
                if is_tile(A):
                    act.wait_ge(x_in[A % 2], nth((A // 2) * 16 + 16))
                    act.wait_ge(stg_done, nth(A * 2 + 2))
                    act.wait_ge(trans_done, nth(A - 1))
                    act.wait_ge(xb_done, nth(A - 1))
                    act.activation(cat[A % 2][:, 0:D], xin[A % 2][:, :], ACT.Relu, bias=stg[A % 4][:, M_OFF:M_OFF + 1],
                                   scale=stg[A % 4][:, M_RSTD:M_RSTD + 1]).then_inc(h_done, 1)
                if T % 4 == 0 and is_chunk(C - HC):
                    first = T - 8
                    act.wait_ge(l2_done, nth((T // 4 - 1) * HC))
                    act.wait_ge(add_done, nth(first + 1))
                    for j in range(BT if (T.coef or T.const < 56) else 1):
                        act.activation(yc[:, j, :], yps[j // 2][:, (j % 2) * D:(j % 2 + 1) * D], ACT.Copy).then_inc(evac_done, 1)
                if is_chunk(C + 1):
                    relu(C + 1)
            steps(act, body)

        @block.tensor
        def _(pe):
            pe.wait_ge(f_row, 1)
            pe.wait_ge(consts, 11)
            pe.matmul(tps[:, 0:NROW], ones[0:1, :], ff, start=True, stop=True).then_inc(f_ps, 1)
            pe.wait_ge(c_in, 64)
            for m in range(HC):
                last = pe.matmul(tpr[:, m:m + 1], w1u[:, m * P:(m + 1) * P], u0[:, :], start=True, stop=True)
            last.then_inc(pe_set, 1)
            pe.wait_ge(ends_ready, 1)
            pe.matmul(l1ps[1][:, 0:NTP], shiftn[:, :], ends[:, 1:NTP + 1], start=True, stop=False)
            pe.matmul(l1ps[1][:, 0:NTP], wrapn[:, :], ends[:, 0:NTP], start=False, stop=True)
            lastn = ident[:, P - 1:P]
            pe.matmul(l1ps[0][0:1, 0:NTP], lastn, ends[:, 0:NTP], start=True, stop=True)
            pe.matmul(sps[1][0:NTP, 0:1], ends[:, 1:NTP + 1], lastn, start=True, stop=True)
            pe.matmul(sps[1][0:NTP, 1:2], ends[:, 0:NTP], lastn, start=True, stop=True).then_inc(pe_set, 1)
            pe.wait_ge(dcol_ready, 1)
            pe.transpose(sps[0][0:NTP, 0:P], Dg[:, :], ident[:, :]).then_inc(pe_set, 1)
            pe.wait_ge(dcol_ready, 2)
            for i, (col, m) in enumerate(((1, ident), (1, trisb), (4, ident), (5, ident))):
                pe.matmul(l1ps[0][0:1, i * 64:i * 64 + NTP], dm[:, col:col + 1], m[0:NTP, 0:NTP], start=True, stop=True)
            pe.matmul(sps[0][0:1, 0:2], onesc[:, :], bad[:, :], start=True, stop=True).then_inc(pe_set, 1)
            pe.wait_ge(setup_free, 2)

            def layer1(C):
                b, m = (C // HC) % 2, C % HC
                cols = columns(C)
                pe.wait_ge(hi_done, nth((C - 1) * 2))
                first = True
                ms = slice(m * P, (m + 1) * P)
                for c in range(KC):
                    for wt, it in ((w1h, inh), (w1l, inh), (w1h, inl)):
                        pe.matmul(l1ps[C % 2][:, 0:cols], wt[:, c, ms], it[b][:, c, 0:cols], start=first, stop=False)
                        first = False
                pe.matmul(l1ps[C % 2][:, 0:cols], w1r[:, ms], inr[b][:, 0:cols], start=False, stop=True).then_inc(l1_done, 1)

            def layer2(C):
                m, cols = C % HC, columns(C)
                pe.wait_ge(lo_done, nth(C + 1))
                if m == 0:
                    pe.wait_ge(evac_done, nth((C // HC) * 4))
                for j in range(cols // P):
                    for ht, wt in ((hh, w2h), (hh, w2l), (hl, w2h)):
                        last = pe.matmul(yps[j // 2][:, (j % 2) * D:(j % 2 + 1) * D], ht[C % 2][:, j * P:(j + 1) * P], wt[:, m, :],
                                         start=(m == 0 and j % 2 == 0 and ht is hh and wt is w2h), stop=(m == HC - 1 and ht is hl),
                                         skip_group_check=True)
                last.then_inc(l2_done, 1)

            def body(T):
                C = (T - 4) * 2
                if is_chunk(C - 2):
                    layer2(C - 2)
                if is_chunk(C):
                    if C % HC == 0:
                        n = T if (T.coef or T.const < 52) else Step(NT)
                        pe.wait_ge(loT_done, nth(n))
                    layer1(C)
                if is_chunk(C - 1):
                    layer2(C - 1)
                if is_tile(T):
                    pe.wait_ge(out2_done, nth(T + 1))
                    pe.wait_ge(outs_done, nth(T + 1))
                    pe.wait_ge(loT_done, nth(T))
                    for c in range(KC):
                        pe.transpose(tps[:, c * P:(c + 1) * P], cat[T % 2][:, c * P:(c + 1) * P], ident[:, :])
                    pe.transpose(tpr[0:3 * KR, 0:P], cat[T % 2][:, KC * P:CAT], ident[:, :]).then_inc(trans_done, 1)
                if is_chunk(C + 1):
                    layer1(C + 1)
                A = T + 1
                if is_tile(A):
                    pe.wait_ge(oh_done, nth(A + 1))
                    pe.wait_ge(nlo_dve, nth(A + 1))
                    pe.wait_ge(nlo_pool, nth(A + 1))
                    pe.wait_ge(joined, nth(A - 1))
                    for j in range(NJ):
                        last = pe.matmul(sps[A % 2][:, 0:2 * F], onehot[A % 2][:, j, :], nhl[:, j, :], start=(j == 0), stop=(j == NJ - 1))
                    last.then_inc(sums_done, 1)
            steps(pe, body)

        @block.vector
        def _(dve):
            set_step = itertools.count(1)
            V = dve
            V.sem_inc(x_used, 1)
            V.sem_inc(g_used, 1)
            dve.wait_ge(consts, 11)
            V.tensor_scalar(out=ident[:, :], in0=iota[:, :], scalar1=pid[:, 0:1], scalar2=None, op0=ALU.is_equal).then_inc(dve_set, 1)
            dve.wait_ge(dve_set, next(set_step))
            V.tensor_scalar(out=pid1[:, :], in0=pid[:, :], scalar1=1.0, scalar2=None, op0=ALU.add).then_inc(dve_set, 1)
            dve.wait_ge(dve_set, next(set_step))
            V.tensor_scalar(out=trisb[:, :], in0=iota[0:NTP, 0:NTP], scalar1=pid[0:NTP, 0:1], scalar2=None, op0=ALU.is_gt).then_inc(dve_set, 1)
            dve.wait_ge(dve_set, next(set_step))
            V.tensor_scalar(out=thr[:, :], in0=iota16[0:NTP, 0:XR], scalar1=float(XW), scalar2=float(2 * WIN), op0=ALU.mult, op1=ALU.add)
            V.tensor_scalar(out=shiftn[:, :], in0=iota[:, :], scalar1=pid1[:, :], scalar2=None, op0=ALU.is_equal)
            V.tensor_scalar(out=wrapn[:, :], in0=iota[:, :], scalar1=pid[:, :], scalar2=float(1 - P), op0=ALU.subtract, op1=ALU.is_equal).then_inc(dve_set, 1)
            dve.wait_ge(dve_set, next(set_step))
            dve.wait_ge(f_in, 16)
            V.tensor_copy(ff, fi).then_inc(f_row, 1)
            dve.wait_ge(f_ps, 1)
            V.tensor_copy(fb, tps[:, 0:NROW]).then_inc(dve_set, 1)
            dve.wait_ge(dve_set, next(set_step))
            V.tensor_scalar(out=nidh[:, :], in0=nid, scalar1=0.5, scalar2=None, op0=ALU.add).then_inc(nid_half, 1)
            group, done = 1, 0
            for i in range(NTP + LAG):
                if i % 2 == 0 and i < NTP:
                    dve.wait_ge(cnt1_done, nth(i // 2 - 1))
                    dve.wait_ge(rowbuf_used, nth((i - 2 - LAG) // 2 + 1))
                    V.tensor_scalar(out=junk[i // 2 % 2][:, 0:NROW], in0=fb, scalar1=nid[:, i:i + 1], scalar2=0.0, op0=ALU.is_le, op1=ALU.add,
                                    accum_out=cnt1[:, i:i + 1]).then_inc(cnt1_done, 1)
                if i + 1 == GROUPS[min(group, len(GROUPS) - 1)]:
                    g, odd = slice(GROUPS[group - 1], i + 1), slice(GROUPS[group - 1] + 1, i + 1, 2)
                    group += 1
                    dve.wait_ge(cnt1_done, i // 2 + 1)
                    dve.wait_ge(cnt1_act, (i + 1) // 2)
                    V.tensor_scalar(out=cnt1[:, odd], in0=cnt1[:, odd], scalar1=0.5, scalar2=NROW / 2, op0=ALU.mult, op1=ALU.add).then_inc(dve_set, 1)
                    dve.wait_ge(dve_set, next(set_step))
                    V.tensor_scalar(out=small[2][:, g], in0=cnt1[:, g], scalar1=1.0, scalar2=-1.0, op0=ALU.max, op1=ALU.add).then_inc(dve_set, 1)
                    dve.wait_ge(dve_set, next(set_step))
                    V.tensor_copy(rowi[:, g], small[2][:, g]).then_inc(row_done, 1)
                t = i - LAG
                if t >= 0 and t % 2 == 0:
                    dve.wait_ge(rowbuf_in[t % RB], 16 * (t // RB + 1))
                    dve.wait_ge(rowbuf_used, nth(t // 2 - 1))
                    dve.wait_ge(cnt1_done, min(i, NTP) // 2)
                    V.tensor_scalar(out=junk[(t // 2 + 1) % 2][:, 0:ROW], in0=rows[t % RB], scalar1=nid[:, t:t + 1], scalar2=0.0, op0=ALU.is_le, op1=ALU.add,
                                    accum_out=cnt2[:, t:t + 1]).then_inc(rowbuf_used, 1)
                if i in (16, 17):
                    c = (i - 16) * 2
                    dve.wait_ge(act_set, i - 15)
                    V.tensor_tensor(out=w1l[:, c:c + 2, :], in0=rawf[c // 2].rearrange("p (c h) -> p c h", h=H), in1=w1h[:, c:c + 2, :], op=ALU.subtract).then_inc(lo_set, 1)
                if i == 18:
                    dve.wait_ge(act_set, KC // 2 + 1)
                    V.tensor_tensor(out=w1r[KR:2 * KR, :], in0=natf[0][KR:2 * KR, 0:H], in1=w1r[KR:2 * KR, :], op=ALU.subtract).then_inc(lo_set, 1)
                if i in (22, 23):
                    c = i - 22
                    dve.wait_ge(act_set, KC // 2 + 2 + c)
                    V.tensor_tensor(out=w2l[:, c * 4:(c + 1) * 4, :], in0=hfw[c], in1=w2h[:, c * 4:(c + 1) * 4, :], op=ALU.subtract).then_inc(lo_set, 1)
                if i == 19:
                    dve.wait_ge(sd_in, 32)
                    V.tensor_tensor(out=sbad[0:SR, :], in0=sd[0:SR, 0:SC], in1=sd[0:SR, 1:SC + 1], op=ALU.is_gt).then_inc(sd_done, 1)
                if i == 21:
                    dve.wait_ge(sd_done, 1)
                    V.tensor_reduce(out=bad[0:SR, 1:2], in_=sbad[0:SR, :], axis=AX.X, op=ALU.max)
                    dve.wait_ge(pe_set, 1)
                    V.tensor_tensor(out=b1e[:, :], in0=tpr[:, 0:HC], in1=b1c[:, :], op=ALU.add)
                while done < min(NT, (i - 20) * 3 // 2):
                    g = done // XG
                    if done % XG == 0:
                        dve.wait_ge(xs_in[g % 2], 16 * (g // 2 + 1) + (16 if g == XGF - 1 else 0))
                    V.bn_stats(out=stats[:, done, :], in_=xs[g % 2][:, done % XG, :]).then_inc(xs_used, 1)
                    done += 1
                    if done % XG == 0:
                        dve.wait_ge(xs_used, done)
                        for q in range(done - XG, done):
                            last = V.bn_aggr(out=mv[:, q, :], in_=stats[:, q, :])
                        if done == NT:
                            last.then_inc(dve_set, 1)
                if i == NTP + 6:
                    dve.wait_ge(dve_set, next(set_step))
                    V.tensor_scalar(out=small[8][:, 0:NT], in0=mv[:, 0:NT, 1], scalar1=EPS, scalar2=None, op0=ALU.add).then_inc(var_ready, 1)
            assert done == NT
            dve.wait_ge(rowbuf_used, (NTP + 1) // 2)
            dve.wait_ge(rowbuf_act, NTP // 2)
            V.tensor_scalar(out=cnt2[:, 1::2], in0=cnt2[:, 1::2], scalar1=0.5, scalar2=ROW / 2, op0=ALU.mult, op1=ALU.add).then_inc(dve_set, 1)
            dve.wait_ge(dve_set, next(set_step))
            V.scalar_tensor_tensor(out=ends[:, 1:NTP + 1], in0=small[2][:, :], scalar=float(ROW), in1=cnt2[:, :], op0=ALU.mult, op1=ALU.add).then_inc(ends_ready, 1)
            E, B, W2nd, tr = ends[:, 1:NTP + 1], small[3], small[6], small[5]
            lev = [tab[:, :, M_B + i] for i in range(4)]
            starts = [small[1], small[6]]
            r0, a, v = small[2][:, 0:NT], small[0][:, 0:NT], small[8][:, 0:NT]
            dve.wait_ge(ends_ready, 1)
            dve.wait_ge(pe_set, 2)
            V.tensor_copy(B[:, :], l1ps[1][:, 0:NTP])
            V.tensor_copy(dm[:, 6:8], sps[1][0:NTP, 0:2])
            V.tensor_scalar(out=small[1][0:1, :], in0=l1ps[0][0:1, 0:NTP], scalar1=float(NE - CAPE), scalar2=None, op0=ALU.min).then_inc(dve_set, 1)
            dve.wait_ge(dve_set, next(set_step))
            V.tensor_tensor(out=Dg[:, :], in0=E, in1=B[:, :], op=ALU.subtract).then_inc(dcol_ready, 1)
            V.tensor_copy(e0row[:, :], small[1][0:1, :]).then_inc(e0_ready, 1)
            V.tensor_scalar(out=dm[:, 4:5], in0=dm[:, 6:7], scalar1=float(NE - WIN), scalar2=None, op0=ALU.is_gt)
            V.tensor_scalar(out=dm[:, 2:3], in0=dm[:, 7:8], scalar1=float(NE - CAPE), scalar2=float(CAPE), op0=ALU.min, op1=ALU.add)
            V.tensor_scalar(out=tab[:, :, M_E8], in0=E, scalar1=float(-XW), scalar2=None, op0=ALU.add)
            V.tensor_copy(tab[:, :, M_S], B[:, :])
            V.tensor_scalar(out=W2nd[:, :], in0=E, scalar1=-1.0, scalar2=None, op0=ALU.add).then_inc(dve_set, 1)
            dve.wait_ge(dve_set, next(set_step))
            V.tensor_tensor(out=dm[:, 3:4], in0=dm[:, 6:7], in1=dm[:, 2:3], op=ALU.is_gt)
            V.tensor_scalar(out=tab[:, :, M_ANY], in0=Dg[:, :], scalar1=1.0, scalar2=None, op0=ALU.min)
            V.tensor_scalar(out=small[0][:, :], in0=Dg[:, :], scalar1=1.0, scalar2=None, op0=ALU.max)
            for i in range(4):
                V.tensor_scalar(out=lev[i], in0=Dg[:, :], scalar1=float(WIN >> i), scalar2=None, op0=ALU.is_ge)
            V.tensor_scalar(out=tab[:, :, M_XB], in0=Dg[:, :], scalar1=float(2 * WIN), scalar2=2.0, op0=ALU.is_gt, op1=ALU.mult).then_inc(dve_set, 1)
            dve.wait_ge(dve_set, next(set_step))
            dve.wait_ge(pe_set, 3)
            V.tensor_reduce(out=dm[:, 0:1], in_=sps[0][0:NTP, 0:P], axis=AX.X, op=ALU.max)
            V.reciprocal(tab[:, :, M_RCNT], small[0][:, :])
            V.tensor_scalar(out=tab[:, :, M_XB], in0=tab[:, :, M_XB], scalar1=-1.0, scalar2=FMAX, op0=ALU.add, op1=ALU.mult)
            V.scalar_tensor_tensor(out=W2nd[:, :], in0=lev[0], scalar=float(-(WIN >> 1)), in1=W2nd[:, :], op0=ALU.mult, op1=ALU.add).then_inc(dve_set, 1)
            dve.wait_ge(dve_set, next(set_step))
            V.tensor_scalar(out=thrj[:, :], in0=thr[:, :], scalar1=dm[:, 0:1], scalar2=0.0, op0=ALU.is_lt, op1=ALU.add, accum_out=dm[:, 1:2])
            V.scalar_tensor_tensor(out=bad[0:NTP, 0:1], in0=dm[:, 0:1], scalar=float(2 * WIN + XR * XW), in1=dm[:, 3:4], op0=ALU.is_gt, op1=ALU.add)
            V.scalar_tensor_tensor(out=W2nd[:, :], in0=lev[1], scalar=float(-(WIN >> 2)), in1=W2nd[:, :], op0=ALU.mult, op1=ALU.add).then_inc(dve_set, 1)
            dve.wait_ge(dve_set, next(set_step))
            V.tensor_tensor(out=dm[:, 5:6], in0=dm[:, 1:2], in1=dm[:, 4:5], op=ALU.add).then_inc(dcol_ready, 1)
            V.scalar_tensor_tensor(out=W2nd[:, :], in0=lev[2], scalar=float(-(WIN >> 3)), in1=W2nd[:, :], op0=ALU.mult, op1=ALU.add).then_inc(dve_set, 1)
            dve.wait_ge(dve_set, next(set_step))
            V.scalar_tensor_tensor(out=W2nd[:, :], in0=lev[3], scalar=float(-(WIN >> 4)), in1=W2nd[:, :], op0=ALU.mult, op1=ALU.add)
            V.tensor_scalar(out=starts[0][:, :], in0=B[:, :], scalar1=float(NE - WIN), scalar2=None, op0=ALU.min).then_inc(dve_set, 1)
            dve.wait_ge(dve_set, next(set_step))
            V.tensor_scalar(out=tr[:, :], in0=W2nd[:, :], scalar1=float(NE - WIN), scalar2=None, op0=ALU.is_gt)
            V.tensor_copy(tabi[:, :, 0], starts[0][:, :])
            V.tensor_tensor(out=tab[:, :, M_LO], in0=B[:, :], in1=starts[0][:, :], op=ALU.subtract).then_inc(dve_set, 1)
            dve.wait_ge(dve_set, next(set_step))
            V.tensor_scalar(out=starts[1][:, :], in0=W2nd[:, :], scalar1=float(NE - WIN), scalar2=0.0, op0=ALU.min, op1=ALU.max)
            V.tensor_scalar(out=tab[:, :, M_HI:M_HI + 2], in0=tr[:, :, None].broadcast_to([P, NTP, 2]), scalar1=float(-WIN), scalar2=float(WIN), op0=ALU.mult, op1=ALU.add)
            V.tensor_tensor(out=tab[:, :, M_B:M_B + 4], in0=tab[:, :, M_B:M_B + 4], in1=tr[:, :, None].broadcast_to([P, NTP, 4]), op=ALU.max).then_inc(dve_set, 1)
            dve.wait_ge(dve_set, next(set_step))
            V.tensor_copy(tabi[:, :, 1], starts[1][:, :])
            V.tensor_tensor(out=tab[:, :, M_LO + 1], in0=B[:, :], in1=starts[1][:, :], op=ALU.subtract)
            V.tensor_scalar(out=tab[:, :, M_B:M_B + 4], in0=tab[:, :, M_B:M_B + 4], scalar1=2.0, scalar2=-1.0, op0=ALU.mult, op1=ALU.add).then_inc(dve_set, 1)
            dve.wait_ge(dve_set, next(set_step))
            for w in range(2):
                V.tensor_tensor(out=starts[w][:, :], in0=E, in1=starts[w][:, :], op=ALU.subtract)
            V.tensor_tensor(out=tab[:, :, M_LO:M_LO + 2], in0=tab[:, :, M_LO:M_LO + 2], in1=tr[:, :, None].broadcast_to([P, NTP, 2]), op=ALU.mult)
            V.tensor_scalar(out=tab[:, :, M_B:M_B + 4], in0=tab[:, :, M_B:M_B + 4], scalar1=FMAX, scalar2=None, op0=ALU.mult).then_inc(dve_set, 1)
            dve.wait_ge(dve_set, next(set_step))
            for w in range(2):
                V.tensor_tensor(out=tab[:, :, M_HI + w], in0=tab[:, :, M_HI + w], in1=starts[w][:, :], op=ALU.max)
            dve.wait_ge(std_ready, 1)
            V.reciprocal(r0, small[7][:, 0:NT])
            V.memset(tab[:, NT:NTP, M_RSTD:M_OFF + 1], 0.0).then_inc(dve_set, 1)
            dve.wait_ge(dve_set, next(set_step))
            dve.wait_ge(pe_set, 4)
            V.tensor_copy(bad[0:1, :], sps[0][0:1, 0:2])
            V.tensor_copy(rcum[:, :, :], l1ps[0][0:1, 0:256].rearrange("p (a b) -> p a b", b=64)[:, :, 0:NTP])
            V.tensor_tensor(out=a, in0=r0, in1=r0, op=ALU.mult).then_inc(dve_set, 1)
            dve.wait_ge(dve_set, next(set_step))
            V.tensor_tensor(out=bad[0:1, 0:1], in0=bad[0:1, 0:1], in1=bad[0:1, 1:2], op=ALU.add)
            V.tensor_tensor(out=a, in0=a, in1=v, op=ALU.mult).then_inc(dve_set, 1)
            dve.wait_ge(dve_set, next(set_step))
            V.tensor_scalar(out=flag[:, :], in0=bad[0:1, 0:1], scalar1=0.5, scalar2=None, op0=ALU.is_gt).then_inc(flag_ready, 1)
            V.tensor_scalar(out=a, in0=a, scalar1=-0.5, scalar2=1.5, op0=ALU.mult, op1=ALU.add).then_inc(dve_set, 1)
            dve.wait_ge(dve_set, next(set_step))
            V.tensor_tensor(out=tab[:, 0:NT, M_RSTD], in0=r0, in1=a, op=ALU.mult).then_inc(dve_set, 1)
            dve.wait_ge(dve_set, next(set_step))
            V.scalar_tensor_tensor(out=tab[:, 0:NT, M_OFF], in0=mv[:, 0:NT, 0], scalar=-1.0, in1=tab[:, 0:NT, M_RSTD], op0=ALU.mult, op1=ALU.mult).then_inc(dve_set, 1)
            dve.wait_ge(dve_set, next(set_step))
            V.sem_inc(setup_free, 1)
            dve.wait_ge(setup_free, 1)
            dve.wait_ge(flag_ready, 1)
            general = dve.value_load(flag[0:1, 0:1], min_val=0, max_val=1)
            with dve.If(general > 0):
                V.memset(eT[F:F + 1, :], 1.0).then_inc(g_upd, 1)
                for p, (rows_, first, op) in enumerate(((F + 1, 0.0, ALU.add), (F, -FMAX, ALU.max))):
                    if p:
                        dve.wait_ge(g_out, 32)
                    V.memset(nodeT[0:rows_, :], first).then_inc(g_upd, 1)
                    with dve.Fori(0, NROW) as r:
                        dve.wait_ge(g_in, r * 32 + (p * NROW * 32 + 32))
                        V.sem_inc(dve_turn, 1)
                        with dve.Fori(0, ROW) as j:
                            n = dve.value_load(gdst[0:1, bass.ds(j, 1)], min_val=0, max_val=N - 1)
                            V.drain()
                            V.tensor_tensor(out=nodeT[0:rows_, bass.ds(n, 1)], in0=nodeT[0:rows_, bass.ds(n, 1)], in1=eT[0:rows_, bass.ds(j, 1)], op=op)
                        V.drain()
                        V.sem_inc(g_used, 1)
                    V.sem_inc(g_done, 1)
                dve.wait_ge(gc_in, 32)
                V.tensor_scalar(out=small[5][:, :], in0=tab[:, :, M_ANY], scalar1=1.0, scalar2=None, op0=ALU.max).then_inc(g_upd, 1)
                dve.wait_ge(g_upd, 4)
                V.reciprocal(tab[:, :, M_RCNT], small[5][:, :]).then_inc(g_upd, 1)
                V.tensor_scalar(out=tab[:, :, M_ANY], in0=tab[:, :, M_ANY], scalar1=1.0, scalar2=None, op0=ALU.min).then_inc(g_upd, 1)
                dve.wait_ge(g_upd, 6)
            V.sem_inc(setup_free, 1)

            def level(M, e, s, i):
                h = WIN >> (i + 1)
                w = e.rearrange("p (w j) f -> p w (j f)", w=2)
                V.scalar_tensor_tensor(out=w[:, :, 0:h * F], in0=w[:, :, h * F:2 * h * F], scalar=s[:, M_B + i:M_B + i + 1],
                                       in1=w[:, :, 0:h * F], op0=ALU.min, op1=ALU.max).then_inc(levels, 1)

            def lo(C):
                cols = columns(C)
                dve.wait_ge(hi_done, nth((C + 1) * 2))
                dve.wait_ge(l2_done, nth(C - 1))
                V.tensor_tensor(out=hl[C % 2][:, 0:cols], in0=hf[C % 2][:, 0:cols], in1=hh[C % 2][:, 0:cols], op=ALU.subtract).then_inc(lo_done, 1)

            def body(T):
                if is_tile(T):
                    dve.wait_ge(sums_done, nth(T + 1))
                    q = sps[T % 2]
                    dve.wait_ge(trans_done, nth(T - 1))
                    V.tensor_reduce(out=cat[T % 2][:, D:D + F], in_=q[:, 0:2 * F].rearrange("p (a f) -> p f a", a=2), axis=AX.X, op=ALU.add).then_inc(joined, 1)
                    dve.wait_ge(gmix, nth(T + 1))
                    V.sem_inc(dve_turn, 1)
                    with dve.If(general > 0):
                        dve.wait_ge(outs_done, nth(T + 1))
                        dve.wait_ge(gt_in, nth(T * 32 + 32))
                        c, rc = cat[T % 2], stg[T % 4][:, M_RCNT:M_RCNT + 1]
                        V.tensor_copy(c[:, D:D + F], gst[:, 0, :])
                        V.tensor_scalar(out=c[:, D + F:D + 2 * F], in0=gst[:, 1, :], scalar1=stg[T % 4][:, M_ANY:M_ANY + 1], scalar2=None, op0=ALU.mult)
                        V.tensor_scalar(out=c[:, D + 2 * F:KC * P], in0=gst[:, 0, 0:F - KR], scalar1=rc, scalar2=None, op0=ALU.mult)
                        V.tensor_scalar(out=c[:, KC * P:CAT].rearrange("p (r k) -> p r k", k=KR), in0=gst[:, 0, None, F - KR:F].broadcast_to([P, 3, KR]),
                                        scalar1=rc, scalar2=None, op0=ALU.mult).then_inc(gt_used, 1)
                        dve.wait_ge(gt_used, nth(T + 1))
                        V.sem_inc(dve_turn, 1)
                    V.sem_inc(out2_done, 1)
                A = T + 2
                if is_tile(A):
                    dve.wait_ge(ndst_in[A % 4], nth((A // 4) * 16 + 16))
                    dve.wait_ge(stg_done, nth(A * 2 + 2))
                    dve.wait_ge(oh_done, nth(A))
                    V.tensor_scalar(out=dloc[:, :], in0=ndst[A % 4][:, :], scalar1=stg[A % 4][:, M_BASE:M_BASE + 1], scalar2=None, op0=ALU.subtract).then_inc(dloc_done, 1)
                    dve.wait_ge(dloc_done, nth(A + 1))
                    dve.wait_ge(sums_done, nth(A - 1))
                    V.tensor_tensor(out=onehot[A % 2][:, :, :], in0=iota[:, None, :].broadcast_to([P, NJ, P]),
                                    in1=dloc[:, :, None].broadcast_to([P, NJ, P]), op=ALU.is_equal).then_inc(oh_done, 1)
                M = T + 1
                e = ell[M % 2]
                s = stg[M % 4]
                if is_tile(M):
                    dve.wait_ge(ell_in[M % 2], nth((M // 2) * 32 + 32))
                    dve.wait_ge(stg_done, nth(M * 2 + 2))
                    extra = dve.value_load(rcum[0:1, 3, bass.ds(M.value, 1)], min_val=0, max_val=XR + 1)
                    with dve.If(extra > 0):
                        past = dve.value_load(rcum[0:1, 2, bass.ds(M.value, 1)], min_val=0, max_val=1)
                        with dve.If(past > 0):
                            dve.wait_ge(gmix, nth(M))
                            V.sem_inc(masked, 1)
                            for w in range(2):
                                V.tensor_scalar(out=wmask[:, w, :], in0=iota16[:, :], scalar1=s[:, M_LO + w:M_LO + w + 1], scalar2=None, op0=ALU.is_ge)
                                V.drain()
                                V.scalar_tensor_tensor(out=wmask[:, w, :], in0=iota16[:, :], scalar=s[:, M_HI + w:M_HI + w + 1], in1=wmask[:, w, :], op0=ALU.is_lt, op1=ALU.mult)
                                V.drain()
                            V.tensor_scalar(out=wmask[:, :, :], in0=wmask[:, :, :], scalar1=2.0, scalar2=-1.0, op0=ALU.mult, op1=ALU.add)
                            V.drain()
                            V.tensor_scalar(out=wmask[:, :, :], in0=wmask[:, :, :], scalar1=FMAX, scalar2=None, op0=ALU.mult)
                            V.drain()
                            V.tensor_tensor(out=e[:, :, :], in0=e[:, :, :], in1=wmask[:, :, :].rearrange("p w j -> p (w j)")[:, :, None].broadcast_to([P, 2 * WIN, F]), op=ALU.min)
                            V.drain()
                        rounds = dve.value_load(rcum[0:1, 0, bass.ds(M.value, 1)], min_val=0, max_val=XR)
                        with dve.If(rounds > 0):
                            before = dve.value_load(rcum[0:1, 1, bass.ds(M.value, 1)], min_val=0, max_val=XR * NTP)
                            with dve.Fori(0, rounds) as q:
                                dve.wait_ge(x_in_w, (before + q) * 16 + 16)
                                V.tensor_reduce(out=mxx[:, :], in_=xw.rearrange("p (j f) -> p f j", f=F), axis=AX.X, op=ALU.max).then_inc(x_red, 1)
                                dve.wait_ge(x_red, before + q + 1)
                                V.scalar_tensor_tensor(out=e[:, 0, :], in0=mxx[:, :], scalar=s[:, M_XB:M_XB + 1], in1=e[:, 0, :], op0=ALU.min, op1=ALU.max).then_inc(x_used, 1)
                                dve.wait_ge(x_used, before + q + 2)
                                V.sem_inc(dve_turn, 1)
                    level(M, e, s, 0)
                if is_tile(M):
                    dve.wait_ge(nhi_done, nth(M + 1))
                    V.tensor_tensor(out=natl[:, 0:JD, :], in0=nat[M % 2][:, 0:JD, :], in1=nath[:, 0:JD, :], op=ALU.subtract).then_inc(nlo_dve, 1)
                C = (T - 4) * 2
                if is_chunk(C):
                    lo(C)
                if is_tile(M):
                    for i in range(1, 4):
                        dve.wait_ge(levels, nth(M * 4 + i))
                        level(M, e, s, i)
                    dve.wait_ge(levels, nth(M * 4 + 4))
                    V.tensor_tensor(out=e[:, 0, :], in0=e[:, 0, :], in1=e[:, WIN, :], op=ALU.max).then_inc(max2, 1)
                    dve.wait_ge(max2, nth(M + 1))
                    dve.wait_ge(trans_done, nth(M - 1))
                    V.tensor_scalar(out=cat[M % 2][:, D + F:D + 2 * F], in0=e[:, 0, :], scalar1=s[:, M_ANY:M_ANY + 1], scalar2=None, op0=ALU.mult).then_inc(gmix, 1)
                if is_tile(T):
                    b, k = (T // 4) % 2, T % 4
                    ks = slice(k * P, (k + 1) * P)
                    dve.wait_ge(hiT_done, nth(T * 2 + 2))
                    V.tensor_tensor(out=inl[b][:, :, ks], in0=tps[:, :].rearrange("p (c n) -> p c n", n=P), in1=inh[b][:, :, ks], op=ALU.subtract)
                    V.tensor_tensor(out=inr[b][2 * KR:3 * KR, ks], in0=tpr[2 * KR:3 * KR, 0:P], in1=inr[b][2 * KR:3 * KR, ks], op=ALU.subtract).then_inc(loT_done, 1)
                if is_chunk(C + 1):
                    lo(C + 1)
            steps(dve, body)


_INS = ["x", "dst", "edge_attr_96", "L0_gnn_u", "L0_gnn_W1", "L0_gnn_b1", "L0_gnn_W2", "L0_gnn_b2"]


def kernel(**inputs):
    import numpy as _np
    import concourse.bacc as _bacc
    from concourse import mybir as _mybir
    from concourse.bass_utils import run_bass_kernel_spmd as _run

    nc = _bacc.Bacc("TRN2", target_bir_lowering=False, num_devices=1)
    arrays, args = {}, []
    for name in _INS:
        a = _np.ascontiguousarray(inputs[name])
        arrays[f"in_{name}"] = a
        args.append(nc.dram_tensor(f"in_{name}", a.shape, _mybir.dt.from_np(a.dtype), kind="ExternalInput").ap())
    shape = inputs["x"].shape
    args.append(nc.dram_tensor("out_y", shape, _mybir.dt.float32, kind="ExternalOutput").ap())
    gnn_block(nc, *args)
    r = _run(nc, [arrays], core_ids=[0])
    return r.results[0]["out_y"]
```
